# Optimizing a Trainium2 kernel written in Bass

```python
import numpy as np
import jax
import jax.numpy as jnp

def _softmax(x, axis=-1):
    return jax.nn.softmax(x, axis=axis)

def _gelu(x):
    return jax.nn.gelu(x, approximate=True)

def _silu(x):
    return jax.nn.silu(x)

def _sigmoid(x):
    return jax.nn.sigmoid(x)

def _layernorm(x, axis=-1, eps=1e-05):
    m = jnp.mean(x, axis=axis, keepdims=True)
    v = jnp.var(x, axis=axis, keepdims=True)
    return (x - m) / jnp.sqrt(v + eps)

def _scatter_add(tgt, idx, src, axis=0):
    return tgt.at[idx].add(src)

def _segment_sum(src, seg, n):
    return jax.ops.segment_sum(src, seg, n)
kernel_name = 'mk_prb_d1_jaxref_r4_f51648'

def setup_inputs(seed: int=0):
    np.random.seed(seed)
    _w = jnp.asarray

    def _L0_attn_setup():
        import jax, jax.numpy as jnp
        import numpy as np
        D_MODEL = 256
        NHEAD = 16
        HEAD_DIM = D_MODEL // NHEAD
        LN_EPS = 1e-05
        ROPE_BASE = 10000.0

        def _rope_cos_sin(n, head_dim):
            inv_freq = 1.0 / ROPE_BASE ** (jnp.arange(0, head_dim, 2, dtype=jnp.float32) / head_dim)
            t = jnp.arange(n, dtype=jnp.float32)
            freqs = jnp.outer(t, inv_freq)
            return (jnp.cos(freqs), jnp.sin(freqs))

        def _apply_rope(x, cos, sin):
            B, H, N, hd = x.shape
            xr = x.reshape(B, H, N, hd // 2, 2)
            x0, x1 = (xr[..., 0], xr[..., 1])
            c = cos[None, None]
            s = sin[None, None]
            rot = jnp.stack([x0 * c - x1 * s, x0 * s + x1 * c], axis=-1)
            return rot.reshape(B, H, N, hd)
        key = jax.random.key(seed)
        ks = jax.random.split(key, 6)
        D = D_MODEL
        scale = 1.0 / np.sqrt(D)
        x = jax.random.normal(ks[0], (2, 512, D), dtype=jnp.float32)
        Wq = jax.random.normal(ks[1], (D, D), dtype=jnp.float32) * scale
        Wk = jax.random.normal(ks[2], (D, D), dtype=jnp.float32) * scale
        Wv = jax.random.normal(ks[3], (D, D), dtype=jnp.float32) * scale
        Wo = jax.random.normal(ks[4], (D, D), dtype=jnp.float32) * scale
        bq = jnp.zeros((D,), jnp.float32)
        bk = jnp.zeros((D,), jnp.float32)
        bv = jnp.zeros((D,), jnp.float32)
        bo = jnp.zeros((D,), jnp.float32)
        ln_w = jnp.ones((D,), jnp.float32)
        ln_b = jnp.zeros((D,), jnp.float32)
        return {'x': x, 'ln_w': ln_w, 'ln_b': ln_b, 'Wq': Wq, 'bq': bq, 'Wk': Wk, 'bk': bk, 'Wv': Wv, 'bv': bv, 'Wo': Wo, 'bo': bo}
    _L0_attn_in = _L0_attn_setup()

    def _L0_ffn_setup():
        import jax, jax.numpy as jnp
        import numpy as np
        B, S, D = (4, 1024, 256)
        E, I = (8, 512)
        CAPACITY = 2
        K = max(1, int(S / E * CAPACITY))
        key = jax.random.key(seed)
        k1, k2, k3, k4, k5 = jax.random.split(key, 5)
        x = jax.random.normal(k1, (B, S, D), dtype=jnp.float32)
        gate_w = jax.random.normal(k2, (D, E), dtype=jnp.float32) * 0.006
        Wg = jax.random.normal(k3, (E, D, I), dtype=jnp.float32) * 0.02
        Wu = jax.random.normal(k4, (E, D, I), dtype=jnp.float32) * 0.02
        Wd = jax.random.normal(k5, (E, I, D), dtype=jnp.float32) * 0.02
        return {'x': x, 'gate_w': gate_w, 'Wg': Wg, 'Wu': Wu, 'Wd': Wd}
    _L0_ffn_in = _L0_ffn_setup()
    _d = {'L0_attn_x': _L0_attn_in['x'], 'L0_attn_ln_w': _L0_attn_in['ln_w'], 'L0_attn_ln_b': _L0_attn_in['ln_b'], 'L0_attn_Wq': _L0_attn_in['Wq'], 'L0_attn_bq': _L0_attn_in['bq'], 'L0_attn_Wk': _L0_attn_in['Wk'], 'L0_attn_bk': _L0_attn_in['bk'], 'L0_attn_Wv': _L0_attn_in['Wv'], 'L0_attn_bv': _L0_attn_in['bv'], 'L0_attn_Wo': _L0_attn_in['Wo'], 'L0_attn_bo': _L0_attn_in['bo'], 'L0_ffn_gate_w': _L0_ffn_in['gate_w'], 'L0_ffn_Wg': _L0_ffn_in['Wg'], 'L0_ffn_Wu': _L0_ffn_in['Wu'], 'L0_ffn_Wd': _L0_ffn_in['Wd']}
    _x0 = _d['L0_attn_x']
    _d['L0_attn_x'] = jax.random.normal(jax.random.fold_in(jax.random.key(seed), 1), (8, 1024, 256), dtype=_x0.dtype)
    del _x0
    return _d

def reference(L0_attn_x, L0_attn_ln_w, L0_attn_ln_b, L0_attn_Wq, L0_attn_bq, L0_attn_Wk, L0_attn_bk, L0_attn_Wv, L0_attn_bv, L0_attn_Wo, L0_attn_bo, L0_ffn_gate_w, L0_ffn_Wg, L0_ffn_Wu, L0_ffn_Wd):

    def _L0_attn_ref(x, ln_w, ln_b, Wq, bq, Wk, bk, Wv, bv, Wo, bo):
        import jax, jax.numpy as jnp
        import numpy as np
        D_MODEL = 256
        NHEAD = 16
        HEAD_DIM = D_MODEL // NHEAD
        LN_EPS = 1e-05
        ROPE_BASE = 10000.0

        def _rope_cos_sin(n, head_dim):
            inv_freq = 1.0 / ROPE_BASE ** (jnp.arange(0, head_dim, 2, dtype=jnp.float32) / head_dim)
            t = jnp.arange(n, dtype=jnp.float32)
            freqs = jnp.outer(t, inv_freq)
            return (jnp.cos(freqs), jnp.sin(freqs))

        def _apply_rope(x, cos, sin):
            B, H, N, hd = x.shape
            xr = x.reshape(B, H, N, hd // 2, 2)
            x0, x1 = (xr[..., 0], xr[..., 1])
            c = cos[None, None]
            s = sin[None, None]
            rot = jnp.stack([x0 * c - x1 * s, x0 * s + x1 * c], axis=-1)
            return rot.reshape(B, H, N, hd)
        B, N, D = x.shape
        H, hd = (NHEAD, HEAD_DIM)
        mu = jnp.mean(x, axis=-1, keepdims=True)
        var = jnp.mean(jnp.square(x - mu), axis=-1, keepdims=True)
        xn = (x - mu) * jax.lax.rsqrt(var + LN_EPS) * ln_w + ln_b

        def proj(W, b):
            return (xn @ W.T + b).reshape(B, N, H, hd).transpose(0, 2, 1, 3)
        q = proj(Wq, bq)
        k = proj(Wk, bk)
        v = proj(Wv, bv)
        cos, sin = _rope_cos_sin(N, hd)
        q = _apply_rope(q, cos, sin)
        k = _apply_rope(k, cos, sin)
        scores = jnp.einsum('bhqd,bhkd->bhqk', q, k) / jnp.sqrt(jnp.float32(hd))
        attn = jax.nn.softmax(scores, axis=-1)
        out = jnp.einsum('bhqk,bhkd->bhqd', attn, v)
        out = out.transpose(0, 2, 1, 3).reshape(B, N, D)
        return x + out @ Wo.T + bo

    def _L0_ffn_ref(x, gate_w, Wg, Wu, Wd):
        import jax, jax.numpy as jnp
        import numpy as np
        B, S, D = (4, 1024, 256)
        E, I = (8, 512)
        CAPACITY = 2
        K = max(1, int(S / E * CAPACITY))
        logits = jnp.einsum('bsd,de->bse', x, gate_w)
        affinity = jax.nn.softmax(logits, axis=-1)
        affinity_T = jnp.transpose(affinity, (0, 2, 1))
        gating, index = jax.lax.top_k(affinity_T, K)
        b_idx = jnp.arange(x.shape[0])[:, None, None]
        x_sel = x[b_idx, index]
        g = jnp.einsum('bekd,edi->beki', x_sel, Wg)
        u = jnp.einsum('bekd,edi->beki', x_sel, Wu)
        h = jax.nn.silu(g) * u
        out = jnp.einsum('beki,eid->bekd', h, Wd)
        contrib = out * gating[..., None]
        x_out = jnp.zeros_like(x).at[b_idx, index].add(contrib)
        return x_out
    x = L0_attn_x
    xn = _layernorm(x, axis=-1)
    x = x + _L0_attn_ref(xn, L0_attn_ln_w, L0_attn_ln_b, L0_attn_Wq, L0_attn_bq, L0_attn_Wk, L0_attn_bk, L0_attn_Wv, L0_attn_bv, L0_attn_Wo, L0_attn_bo) + _L0_ffn_ref(xn, L0_ffn_gate_w, L0_ffn_Wg, L0_ffn_Wu, L0_ffn_Wd)
    return x

_drawn_inputs = setup_inputs


def setup_inputs(seed=0):
    import zlib

    import numpy as np

    out = dict(_drawn_inputs(seed))
    spreads = {'L0_attn_ln_w': (1.0, 0.6),
     'L0_attn_ln_b': (0.0, 0.43),
     'L0_attn_bq': (0.0, 0.8),
     'L0_attn_bk': (0.0, 0.8),
     'L0_attn_bv': (0.0, 0.537),
     'L0_attn_bo': (0.0, 0.538)}
    factors = {'L0_ffn_gate_w': 8.0, 'L0_ffn_Wg': 8.0, 'L0_ffn_Wu': 8.0, 'L0_ffn_Wd': 8.0}
    for name, (base, spread) in spreads.items():
        noise = np.random.default_rng([zlib.crc32(name.encode()), seed]).standard_normal(out[name].shape)
        drawn = base * np.exp(spread * noise) if base else spread * noise
        out[name] = jnp.asarray(drawn.astype(out[name].dtype))
    for name, factor in factors.items():
        out[name] = (out[name] * factor).astype(out[name].dtype)
    return out
```

```python
from contextlib import ExitStack

import concourse.bass as bass
from concourse import mybir

ACT = mybir.ActivationFunctionType
ALU = mybir.AluOpType
AX_X = mybir.AxisListType.X
F32 = mybir.dt.float32
F32R = mybir.dt.float32r
BF16 = mybir.dt.bfloat16
U32 = mybir.dt.uint32

P = 128
LN_EPS = 1e-5
NHEAD = 16
NEXPERT = 8
DMA = 16
HPG = 4
KEYS_W = 32
NPART = 3

Q_PARTS = (0, 0, 1, 1, 0, 2)
K_PARTS = (0, 1, 0, 1, 2, 0)


class Tally:

    def __init__(self, sem, per):
        self.sem, self.per, self.base, self.count = sem, per, 0, 0

    def start(self, n):
        self.base, self.count = n * self.per, 0

    def mark(self, instruction):
        instruction.then_inc(self.sem, 1)
        self.count += 1
        assert self.count <= self.per

    def settle(self, eng, wait=None):
        if wait:
            wait(eng, self.sem, self.base + self.count)
        else:
            eng.wait_ge(self.sem, self.base + self.count)

    def end(self):
        assert self.count == self.per, (self.count, self.per)


def build(nc, x, ln_w, ln_b, wq_t, wk_t, wv_t, wo_t, bq, bk, bv, bo, gate_w, wg, wu, wd,
          cos, sin, ident, row0, out):
    T, D = x.shape
    NB = 8
    S = T // NB
    TT = S // P
    DC = D // P
    HALF = S // 2
    HT = HALF // P
    HD = D // NHEAD
    HR = HD // 2
    NG = NHEAD // HPG
    KT = S // P
    STEPS = NG * 2 * KT
    ROWS = len(Q_PARTS) * HD
    SHIFT = ROWS
    FULL = ROWS + NPART
    SCALE = float(HD) ** -0.5
    E = NEXPERT
    CAP = 2 * S // E
    BE = NB * E
    F = wg.shape[2]
    FC = F // P

    q_dram = nc.dram_tensor("q_parts", (NB, NPART, NHEAD, 2, HR, S), BF16).ap()
    k_dram = nc.dram_tensor("k_parts", (NB, NPART, NHEAD, 2, HR, S), BF16).ap()
    shift_dram = nc.dram_tensor("shift_parts", (NB, NG, NPART, HPG * KT, P), BF16).ap()
    o_dram = nc.dram_tensor("o_sums", (NB, 2, NG, HPG, 2, HD, HALF), F32).ap()
    xn_dram = nc.dram_tensor("xn_rows", (T, D), F32).ap()

    outer = ExitStack()
    with outer:
        def sem(name):
            return outer.enter_context(nc.semaphore(name))

        def keep(name, shape, dt):
            return outer.enter_context(nc.sbuf_tensor(name, shape, dt))

        ident_sb = keep("ident_sb", [P, P], F32)
        row0_sb = keep("row0_sb", [BE, 1], F32)
        affinity = keep("affinity", [P, TT, BE], F32)
        top_gate = keep("top_gate", [BE, CAP], F32)
        top_row = keep("top_row", [BE, CAP], U32)

        with ExitStack() as inner:
            attention_part(nc, inner, locals())
        with ExitStack() as inner:
            expert_part(nc, inner, locals())


def attention_part(nc, ctx, g):
    (T, D, NB, S, TT, DC, HALF, HT, HD, HR, NG, KT, STEPS, ROWS, SHIFT, FULL, SCALE, E, CAP, BE) = (
        g[k] for k in "T D NB S TT DC HALF HT HD HR NG KT STEPS ROWS SHIFT FULL SCALE E CAP BE".split())
    x, out, q_dram, k_dram, shift_dram, o_dram, xn_dram = (
        g[k] for k in "x out q_dram k_dram shift_dram o_dram xn_dram".split())
    ident_sb, row0_sb, affinity, top_gate, top_row = (
        g[k] for k in "ident_sb row0_sb affinity top_gate top_row".split())

    def sb(name, shape, dt=F32):
        return ctx.enter_context(nc.sbuf_tensor(name, shape, dt))

    def ps(name, shape):
        return ctx.enter_context(nc.psum_tensor(name, shape, F32))

    def sem(name):
        return ctx.enter_context(nc.semaphore(name))

    w_hi = [sb(f"w_hi{i}", [P, DC, D], F32R) for i in range(4)]
    w_lo = [sb(f"w_lo{i}", [P, DC, D], F32R) for i in range(4)]
    WQ, WK, WV, WO = range(4)
    cos_sb, sin_sb = sb("cos_sb", [P, S]), sb("sin_sb", [P, S])
    gate_sb = sb("gate_sb", [P, DC, E])
    lnw_sb, lnb_sb = sb("lnw_sb", [P, DC]), sb("lnb_sb", [P, DC])
    bq_sb, bk_sb = sb("bq_sb", [P, 2]), sb("bk_sb", [P, 2])
    bv_sb, bo_sb = sb("bv_sb", [P, D]), sb("bo_sb", [P, D])
    minus_half = sb("minus_half", [P, HT])
    xin, xn, z = (sb(n, [P, HT, D]) for n in ("xin", "xn", "z"))
    stats = sb("stats", [P, HT, 6])
    mv1, mv2 = sb("mv1", [P, HT, 2]), sb("mv2", [P, HT, 2])
    ve1, ve2 = sb("ve1", [P, HT]), sb("ve2", [P, HT])
    rstd1, rstd2 = sb("rstd1", [P, HT]), sb("rstd2", [P, HT])
    xnT = sb("xnT", [P, DC, HALF])
    znT = sb("znT", [P, DC, HALF])
    zn_hi, zn_lo = sb("zn_hi", [P, DC, S], F32R), sb("zn_lo", [P, DC, S], F32R)
    lg_max, lg_sum, lg_rec = (sb(n, [P, HT]) for n in ("lg_max", "lg_sum", "lg_rec"))
    lg, lg_exp = sb("lg", [P, HT, E]), sb("lg_exp", [P, HT, E])
    qk = [sb(f"qk{i}", [P, HALF]) for i in range(4)]
    rot = [sb(f"rot{i}", [P, HALF]) for i in range(8)]
    parts = [sb(f"parts{i}", [P, NPART, 2, HALF], BF16) for i in range(2)]
    v_sb = sb("v_sb", [P, KT, D])
    q_stack = [sb(f"q_stack{i}", [P, HPG, S], BF16) for i in range(2)]
    k_stack = [sb(f"k_stack{i}", [P, HPG, S], BF16) for i in range(2)]
    v_ones = [sb(f"v_ones{i}", [P, KT, HPG, KEYS_W]) for i in range(2)]
    probs = [sb(f"probs{i}", [P, HPG, HALF]) for i in range(2)]
    row_max = sb("row_max", [P, HPG * KT])
    neg_max, neg_rest = sb("neg_max", [HPG * KT, P]), sb("neg_rest", [HPG * KT, P])
    shift = sb("shift", [HPG * KT, NPART, P], BF16)
    o_sb = [sb(f"o_sb{i}", [P, HALF]) for i in range(2)]
    num, den = sb("num", [P, DC, S]), sb("den", [P, DC, S])
    at_hi = [sb(f"at_hi{i}", [P, DC, 2 * P], F32R) for i in range(2)]
    at_lo = [sb(f"at_lo{i}", [P, DC, 2 * P], F32R) for i in range(2)]
    base = sb("base", [P, TT, D])
    top_scores = znT[0:BE, :, :].rearrange("p c n -> p (c n)")

    score = [ps(f"score{i}", [P, 2, HALF]) for i in range(2)]
    o_ps = ps("o_ps", [P, HALF])
    wo_ps = ps("wo_ps", [P, 2, D])
    side = [ps(f"side{i}", [P, HALF]) for i in range(2)]

    const_in, weights_in = sem("const_in"), sem("weights_in")
    ones_set, passed = sem("ones_set"), sem("passed")
    const_set, weights_split, weights_high = sem("const_set"), sem("weights_split"), sem("weights_high")
    x_in, base_out, xn_out = sem("x_in"), sem("base_out"), sem("xn_out")
    stats1_done, stats2_done, rstd1_done, rstd2_done = (
        sem(n) for n in ("stats1_done", "stats2_done", "rstd1_done", "rstd2_done"))
    xn_ready, z_ready = sem("xn_ready"), sem("z_ready")
    side_full, side_free = sem("side_full"), sem("side_free")
    zn_ready, lg_exped, aff_done = sem("zn_ready"), sem("lg_exped"), sem("aff_done")
    parts_ready, parts_out = sem("parts_ready"), sem("parts_out")
    v_ones_ready = sem("v_ones_ready")
    stack_in = [sem(f"stack_in{i}") for i in range(2)]
    max_full, max_free, max_turned = sem("max_full"), sem("max_free"), sem("max_turned")
    shift_ready, shift_out, shift_in = sem("shift_ready"), sem("shift_out"), sem("shift_in")
    qk_done = [sem(f"qk_done{i}") for i in range(2)]
    exp_done = [sem(f"exp_done{i}") for i in range(2)]
    pv_done, o_copied = sem("pv_done"), sem("o_copied")
    o_out = [sem(f"o_out{i}") for i in range(2)]
    sums_in, base_in, y_out = sem("sums_in"), sem("base_in"), sem("y_out")
    at_split, wo_done, y_ready = sem("at_split"), sem("wo_done"), sem("y_ready")
    aff_turned, top_copied = sem("aff_turned"), sem("top_copied")
    dve_a = Tally(sem("dve_a"), 11)
    dve_b = Tally(sem("dve_b"), 4)
    dve_d = Tally(sem("dve_d"), 6)
    dve_t = Tally(sem("dve_t"), 3 * CAP // 8)
    pool_a = Tally(sem("pool_a"), 4)

    CONSTS = 11
    JOBS = 22
    QUARTERS = S // (2 * P)
    PARTS_DMA = 2 * NPART * 2 * DMA

    ROUTER_STEP = (16, 37)
    WO_STEP = (4, 5, 6, 7)
    HALF_STEPS = ((12, 13, 13, 14, 15, 17, 18, 19, 20), (32, 33, 34, 35, 36, 38, 39, 40, 41))
    V_STEP = (46, 48, 50, 52)

    def need(eng, s, value):
        if not isinstance(value, int) or value > 0:
            eng.wait_ge(s, value)

    def hold(eng, s, value):
        need(eng, s, value)
        if not isinstance(value, int):
            eng.sem_inc(passed, 1)

    block = ctx.enter_context(nc.Block())

    @block.sync
    def _(sp):
        consts = ((ident_sb[:, :], g["ident"]), (row0_sb[:, :], g["row0"]),
                  (cos_sb[:, :], g["cos"]), (sin_sb[:, :], g["sin"]),
                  (gate_sb[:, :, :], g["gate_w"].rearrange("(c p) e -> p c e", p=P)),
                  (lnw_sb[:, :], g["ln_w"]),
                  (lnb_sb[:, :], g["ln_b"]),
                  (bq_sb[:, :], g["bq"]),
                  (bk_sb[:, :], g["bk"]),
                  (bv_sb[:, :], g["bv"].partition_broadcast(P)),
                  (bo_sb[:, :], g["bo"].partition_broadcast(P)))
        assert len(consts) == CONSTS
        for i, name in enumerate(("wq_t", "wk_t", "wv_t", "wo_t")):
            sp.dma_start(probs[0][:, i, :].rearrange("p (c n) -> p c n", c=DC),
                         g[name].rearrange("(c p) n -> p c n", p=P)).then_inc(weights_in, DMA)
        for to, of in consts:
            sp.dma_start(to, of).then_inc(const_in, DMA)

        def load_stack(b, hg):
            par = hg % 2
            for r, (qp, kp) in enumerate(zip(Q_PARTS, K_PARTS)):
                for stack, dram, part in ((q_stack[par], q_dram, qp), (k_stack[par], k_dram, kp)):
                    sp.dma_start(stack[r * HD:(r + 1) * HD, :, :],
                                 dram[b, part, hg * HPG:(hg + 1) * HPG].rearrange("h a i n -> (a i) h n"))\
                      .then_inc(stack_in[par], DMA)

        def store_parts(n, th):
            hold(sp, parts_ready, 2 * n + th + 1)
            for src, dram in ((0, q_dram), (1, k_dram)):
                for part in range(NPART):
                    for a in range(2):
                        sp.dma_start(dram[n, part, :, a, :, th * HALF:(th + 1) * HALF],
                                     parts[src][:, part, a, :]).then_inc(parts_out, DMA)

        def shift_rows(b, hg):
            u = b * NG + hg
            hold(sp, shift_ready, u + 1)
            sp.dma_start(shift_dram[b, hg].rearrange("c t n -> t c n"), shift[:, :, :]).then_inc(shift_out, DMA)
            hold(sp, shift_out, DMA * (u + 1))
            sp.dma_start(q_stack[hg % 2][SHIFT:FULL, :, :].rearrange("c h n -> c (h n)"),
                         shift_dram[b, hg].rearrange("c t n -> c (t n)")).then_inc(shift_in, DMA)

        def store_o(b, il):
            i = b * 2 * NG + il
            hold(sp, o_copied, i + 1)
            sp.dma_start(o_dram[b, il % 2, il // 2].rearrange("j w r n -> (j w r) n"),
                         o_sb[il % 2][:, :]).then_inc(o_out[il % 2], DMA)

        def load_sums(d):
            for i in range(2):
                hold(sp, o_out[i], DMA * NG * (d + 1))
            for qh in range(2):
                for c in range(DC):
                    src = o_dram[d, qh, 2 * c:2 * c + 2].rearrange("g j w r n -> w (g j) r n")
                    for w, to in ((0, num), (1, den)):
                        sp.dma_start(to[:, c, qh * HALF:(qh + 1) * HALF], src[w]).then_inc(sums_in, DMA)
            hold(sp, base_out, 2 * DMA * (d + 1))
            rows = out[bass.ds(d * S, S), :].rearrange("(t p) n -> p t n", p=P)
            sp.dma_start(base[:, :, :], rows).then_inc(base_in, DMA)

        def store_y(d):
            rows = out[bass.ds(d * S, S), :].rearrange("(t p) n -> p t n", p=P)
            for hf in range(2):
                hold(sp, y_ready, QUARTERS * d + 2 * hf + 2)
                sp.dma_start(rows[:, hf * HT:(hf + 1) * HT, :], base[:, hf * HT:(hf + 1) * HT, :])\
                  .then_inc(y_out, DMA)

        def first_stack(n):
            hold(sp, parts_out, (n + 1) * 2 * PARTS_DMA)
            load_stack(n, 0)

        def attend(b, nxt, prev):
            hold(sp, exp_done[1], b * STEPS)
            load_stack(b, 1)
            shift_rows(b, 0)
            if prev is not None:
                store_o(prev, 2 * NG - 1)
                load_sums(prev)
                store_y(prev)
            store_o(b, 0)
            hold(sp, exp_done[1], b * STEPS + 2 * KT)
            shift_rows(b, 1)
            load_stack(b, 2)
            store_o(b, 1)
            store_o(b, 2)
            hold(sp, exp_done[1], b * STEPS + 4 * KT)
            shift_rows(b, 2)
            load_stack(b, 3)
            store_o(b, 3)
            if nxt is not None:
                store_parts(nxt, 0)
            if prev is not None:
                hold(sp, y_out, 2 * DMA * (prev + 1))
            store_o(b, 4)
            hold(sp, exp_done[1], b * STEPS + 6 * KT)
            shift_rows(b, 3)
            store_o(b, 5)
            if nxt is not None:
                store_parts(nxt, 1)
                first_stack(nxt)
            store_o(b, 6)

        store_parts(0, 0)
        store_parts(0, 1)
        first_stack(0)
        attend(0, 1, None)
        with sp.Fori(1, NB - 1) as b:
            attend(b, b + 1, b - 1)
        attend(NB - 1, None, NB - 2)
        store_o(NB - 1, 2 * NG - 1)
        load_sums(NB - 1)
        store_y(NB - 1)
        hold(sp, y_out, 2 * DMA * NB)

    @block.gpsimd
    def _(pool):
        pool.memset(minus_half[:, :], -0.5).then_inc(const_set, 1)
        for i in range(2):
            pool.memset(v_ones[i][:, :, :, :], 1.0).then_inc(const_set, 1)

        def norm(n, th):
            u = 2 * n + th
            pool_a.start(u)
            hold(pool, base_out, DMA * u)
            pool.dma_start(xin[:, :, :], x[bass.ds(n * S + th * HALF, HALF), :]
                           .rearrange("(t p) n -> p t n", p=P)).then_inc(x_in, DMA)
            for stats_done, mv, ve, rstd, rstd_done in ((stats1_done, mv1, ve1, rstd1, rstd1_done),
                                                        (stats2_done, mv2, ve2, rstd2, rstd2_done)):
                hold(pool, stats_done, u + 1)
                pool_a.mark(pool.tensor_scalar(ve[:, :], mv[:, :, 1], LN_EPS, None, ALU.add))
                pool_a.settle(pool, hold)
                pool.tensor_tensor(rstd[:, :], ve[:, :], minus_half[:, :], ALU.pow).then_inc(rstd_done, 1)
            out_rows = xn_dram[bass.ds(n * S + th * HALF, HALF), :].rearrange("(t p) n -> p t n", p=P)
            pool.dma_start(out_rows, xn[:, :, :]).then_inc(xn_out, DMA)
            pool_a.mark(pool.tensor_tensor(xin[:, :, :], xin[:, :, :], xn[:, :, :], ALU.add))
            pool_a.settle(pool, hold)
            for t in range(HT):
                last = pool.tensor_tensor(xin[:, t, :], xin[:, t, :], bo_sb[:, :], ALU.add)
            pool_a.mark(last)
            pool_a.settle(pool, hold)
            base_rows = out[bass.ds(n * S + th * HALF, HALF), :].rearrange("(t p) n -> p t n", p=P)
            pool.dma_start(base_rows, xin[:, :, :]).then_inc(base_out, DMA)
            pool_a.end()

        def set_v(b, hg):
            hold(pool, pv_done, (b * NG + hg - 1) * 2 * KT)
            pool.tensor_copy(v_ones[hg % 2][:, :, :, 0:HD],
                             v_sb[:, :, hg * HPG * HD:(hg + 1) * HPG * HD]
                             .rearrange("p t (j d) -> p t j d", j=HPG)).then_inc(v_ones_ready, 1)

        def attend(b, nxt, prev):
            set_v(b, 1)
            if nxt is not None:
                norm(nxt, 0)
            set_v(b, 2)
            if nxt is not None:
                norm(nxt, 1)
            set_v(b, 3)
            if nxt is not None:
                hold(pool, side_free, (nxt + 1) * JOBS)
                set_v(nxt, 0)

        hold(pool, const_in, CONSTS * DMA)
        hold(pool, const_set, 3)
        norm(0, 0)
        norm(0, 1)
        hold(pool, side_free, JOBS)
        set_v(0, 0)
        attend(0, 1, None)
        with pool.Fori(1, NB - 1) as b:
            attend(b, b + 1, b - 1)
        attend(NB - 1, None, NB - 2)
        hold(pool, base_out, 2 * DMA * NB)
        hold(pool, xn_out, 2 * DMA * NB)

    @block.scalar
    def _(act):
        def router(n, th):
            act.wait_ge(side_free, n * JOBS + 9 * th + 5)
            act.activation(lg_exp[:, :, :], lg[:, :, :], ACT.Exp).then_inc(lg_exped, 1)

        def attend(b, nxt, prev):
            for s in range(STEPS):
                at = b * STEPS + s
                for i in range(2):
                    act.wait_ge(qk_done[i], at + 1)
                    if i == 0:
                        need(act, pv_done, at - 1)
                    act.activation(probs[s % 2][:, 2 * i:2 * i + 2, :], score[i][:, :, :], ACT.Exp,
                                   scale=SCALE).then_inc(exp_done[i], 1)
                if nxt is not None and s in ROUTER_STEP:
                    router(nxt, ROUTER_STEP.index(s))

        router(0, 0)
        router(0, 1)
        act.wait_ge(weights_split, 1)
        attend(0, 1, None)
        with act.Fori(1, NB - 1) as b:
            attend(b, b + 1, b - 1)
        attend(NB - 1, None, NB - 2)

    @block.tensor
    def _(pe):
        def open_side(n, job):
            need(pe, side_free, n * JOBS + job - 1)
            return side[job % 2]

        def half_job(n, th, k):
            u, job = 2 * n + th, 9 * th + k
            cols = slice(th * HALF, (th + 1) * HALF)
            bank = open_side(n, job)
            if k < 4:
                src, ready, c = ((xn, xn_ready), (z, z_ready))[k // 2] + (k % 2,)
                pe.wait_ge(ready, u + 1)
                for t in range(HT):
                    last = pe.transpose(bank[:, t * P:(t + 1) * P], src[:, t, c * P:(c + 1) * P], ident_sb[:, :])
            elif k == 4:
                for t in range(HT):
                    for c in range(DC):
                        last = pe.matmul(bank[:, t * E:(t + 1) * E], xnT[:, c, t * P:(t + 1) * P],
                                         gate_sb[:, c, :], start=c == 0, stop=c == DC - 1)
            else:
                w, a = ((WQ, 0), (WQ, 1), (WK, 0), (WK, 1))[k - 5]
                pe.wait_ge(zn_ready, u + 1)
                for i, (wt, zt) in enumerate(PASSES(w)):
                    for c in range(DC):
                        last = pe.matmul(bank[:, :], wt[:, c, a * P:(a + 1) * P], zt[:, c, cols],
                                         start=i == 0 and c == 0, stop=i == 2 and c == DC - 1)
            last.then_inc(side_full, 1)

        def PASSES(w):
            return (w_hi[w], zn_hi), (w_lo[w], zn_hi), (w_hi[w], zn_lo)

        def v_job(n, pair):
            bank = open_side(n, 18 + pair)
            if pair == 0:
                pe.wait_ge(zn_ready, 2 * n + 2)
            for t2 in range(2):
                t = 2 * pair + t2
                for i, (wt, zt) in enumerate(PASSES(WV)):
                    for c in range(DC):
                        last = pe.matmul(bank[:, t2 * D:(t2 + 1) * D], zt[:, c, t * P:(t + 1) * P], wt[:, c, :],
                                         start=i == 0 and c == 0, stop=i == 2 and c == DC - 1)
            last.then_inc(side_full, 1)

        def wo_job(d, quarter):
            pe.wait_ge(at_split, QUARTERS * d + quarter + 1)
            if quarter > 0:
                pe.wait_ge(y_ready, QUARTERS * d + quarter)
            hi, lo = at_hi[quarter % 2], at_lo[quarter % 2]
            for t in range(2):
                for i, (at, wt) in enumerate(((hi, w_hi[WO]), (lo, w_hi[WO]), (hi, w_lo[WO]))):
                    for c in range(DC):
                        last = pe.matmul(wo_ps[:, t, :], at[:, c, t * P:(t + 1) * P], wt[:, c, :],
                                         start=i == 0 and c == 0, stop=i == 2 and c == DC - 1)
            last.then_inc(wo_done, 1)

        def maxima(b, hg):
            u, n = b * NG + hg, HPG * KT
            par = hg % 2
            for k in range(n):
                j, t = k // KT, k % KT
                if k >= 2:
                    pe.wait_ge(max_free, u * n + k - 1)
                for kh in range(2):
                    last = pe.matmul(score[k % 2][:, kh, :], q_stack[par][0:ROWS, j, t * P:(t + 1) * P],
                                     k_stack[par][0:ROWS, j, kh * HALF:(kh + 1) * HALF], start=True, stop=True)
                last.then_inc(max_full, 1)
            pe.wait_ge(max_free, u * n + n)
            pe.transpose(score[0][0:n, 0, 0:P], row_max[:, :], ident_sb[:, :]).then_inc(max_turned, 1)

        def pv(s, g_half=None, group=None):
            par, kt = (s // (2 * KT)) % 2, s % KT
            if kt == 0:
                need(pe, o_copied, g_half)
            if s % (2 * KT) == 0:
                pe.wait_ge(v_ones_ready, group + 1)
            for j in range(HPG):
                last = pe.matmul(o_ps[j * KEYS_W:(j + 1) * KEYS_W, :], v_ones[par][:, kt, j, :],
                                 probs[s % 2][:, j, :], start=kt == 0, stop=kt == KT - 1)
            last.then_inc(pv_done, 1)

        def attend(b, nxt, prev):
            for s in range(STEPS):
                at = b * STEPS + s
                hg, par, qh, kt = s // (2 * KT), (s // (2 * KT)) % 2, (s // KT) % 2, s % KT
                if s % (2 * KT) == 0:
                    pe.wait_ge(stack_in[par], (b * (NG // 2) + hg // 2 + 1) * 2 * len(Q_PARTS) * DMA)
                    if not (isinstance(b, int) and b == 0 and s == 0):
                        for i in range(2):
                            pe.wait_ge(exp_done[i], at)
                        pv((s - 1) % STEPS, None, None)
                    maxima(b, hg)
                    pe.wait_ge(shift_in, (b * NG + hg + 1) * DMA)
                for i in range(2):
                    if s % (2 * KT) != 0:
                        pe.wait_ge(exp_done[i], at)
                    for j in range(2):
                        last = pe.matmul(score[i][:, j, :], k_stack[par][0:FULL, 2 * i + j, kt * P:(kt + 1) * P],
                                         q_stack[par][0:FULL, 2 * i + j, qh * HALF:(qh + 1) * HALF],
                                         start=True, stop=True)
                    last.then_inc(qk_done[i], 1)
                if s % (2 * KT) != 0:
                    pv(s - 1, b * 2 * NG + (s - 1) // KT, b * NG + (s - 1) // (2 * KT))
                if prev is not None and s in WO_STEP:
                    wo_job(prev, WO_STEP.index(s))
                if nxt is not None:
                    for th in range(2):
                        for k in range(9):
                            if HALF_STEPS[th][k] == s:
                                half_job(nxt, th, k)
                    if s in V_STEP:
                        v_job(nxt, V_STEP.index(s))

        pe.wait_ge(const_in, CONSTS * DMA)
        pe.wait_ge(weights_split, 1)
        pe.wait_ge(const_set, 3)
        pe.wait_ge(ones_set, 2)
        for th in range(2):
            for k in range(9):
                half_job(0, th, k)
        for pair in range(4):
            v_job(0, pair)
        attend(0, 1, None)
        with pe.Fori(1, NB - 1) as b:
            attend(b, b + 1, b - 1)
        attend(NB - 1, None, NB - 2)
        pe.wait_ge(exp_done[1], NB * STEPS)
        pv(STEPS - 1)
        for quarter in range(QUARTERS):
            wo_job(NB - 1, quarter)
        pe.wait_ge(aff_done, 2 * NB)
        for t in range(TT):
            last = pe.transpose(score[t // 4][0:BE, (t % 4) // 2, (t % 2) * P:(t % 2 + 1) * P],
                                affinity[:, t, :], ident_sb[:, :])
        last.then_inc(aff_turned, 1)

    @block.vector
    def _(dve):
        def stats_of(n, src, mv, done):
            for t in range(HT):
                last = dve.bn_stats(stats[:, t, :], src[:, t, :])
            dve_a.mark(last)
            dve_a.settle(dve, hold)
            for t in range(HT):
                last = dve.bn_aggr(mv[:, t, :], stats[:, t, :])
            last.then_inc(done, 1)

        def scaled(to, src, mv, rstd, ready=None):
            for t in range(HT):
                last = dve.tensor_scalar(to[:, t, :], src[:, t, :], mv[:, t, 0:1], rstd[:, t:t + 1],
                                         ALU.subtract, ALU.mult)
            last.then_inc(ready, 1)

        def norm1(n, th):
            u = 2 * n + th
            dve_a.start(u)
            dve.wait_ge(x_in, DMA * (u + 1))
            stats_of(n, xin, mv1, stats1_done)

        def norm2(n, th):
            u = 2 * n + th
            dve.wait_ge(rstd1_done, u + 1)
            need(dve, xn_out, DMA * u)
            scaled(xn, xin, mv1, rstd1, xn_ready)
            dve.wait_ge(xn_ready, u + 1)
            stats_of(n, xn, mv2, stats2_done)

        def norm3(n, th):
            dve.wait_ge(rstd2_done, 2 * n + th + 1)
            scaled(z, xn, mv2, rstd2, z_ready)

        def take(n, job):
            dve.wait_ge(side_full, n * JOBS + job + 1)
            return side[job % 2]

        def turned_x(n, th, c):
            job = 9 * th + c
            bank = take(n, job)
            dve.tensor_copy(xnT[:, c, :], bank[:, :]).then_inc(side_free, 1)

        def turned_z(n, th, c):
            bank = take(n, 9 * th + 2 + c)
            dve.tensor_scalar(znT[:, c, :], bank[:, :], lnw_sb[:, c:c + 1], lnb_sb[:, c:c + 1],
                              ALU.mult, ALU.add).then_inc(side_free, 1)
            if c == DC - 1:
                cols = slice(th * HALF, (th + 1) * HALF)
                dve.wait_ge(side_free, n * JOBS + 9 * th + 4)
                dve_a.mark(dve.tensor_copy(zn_hi[:, :, cols], znT[:, :, :]))
                dve_a.settle(dve)
                dve.tensor_tensor(zn_lo[:, :, cols], znT[:, :, :], zn_hi[:, :, cols], ALU.subtract)\
                   .then_inc(zn_ready, 1)

        def logits(n, th):
            bank = take(n, 9 * th + 4)
            view = bank[:, 0:HT * E].rearrange("p (t e) -> p t e", e=E)
            dve_a.mark(dve.tensor_reduce(lg_max[:, :], view, AX_X, ALU.max))
            dve_a.settle(dve)
            dve.tensor_tensor(lg[:, :, :], view, lg_max[:, :].unsqueeze(2).to_broadcast([P, HT, E]),
                              ALU.subtract).then_inc(side_free, 1)

        def affinities(n, th):
            u = 2 * n + th
            dve.wait_ge(lg_exped, u + 1)
            dve_a.mark(dve.tensor_reduce(lg_sum[:, :], lg_exp[:, :, :], AX_X, ALU.add))
            dve_a.settle(dve)
            dve_a.mark(dve.reciprocal(lg_rec[:, :], lg_sum[:, :]))
            dve_a.settle(dve)
            for t in range(HT):
                last = dve.tensor_scalar(affinity[:, th * HT + t, bass.ds(n * E, E)], lg_exp[:, t, :],
                                         lg_rec[:, t:t + 1], None, ALU.mult)
            last.then_inc(aff_done, 1)

        def biased(n, th, k):
            bank = take(n, 9 * th + 5 + k)
            bias = (bq_sb, bk_sb)[k // 2]
            dve.tensor_scalar(qk[k][:, :], bank[:, :], bias[:, k % 2:k % 2 + 1], None, ALU.add)\
               .then_inc(side_free, 1)

        def rotary(n, th):
            cols = slice(th * HALF, (th + 1) * HALF)
            dve.wait_ge(side_free, n * JOBS + 9 * th + 9)
            for s in range(2):
                a, b = qk[2 * s], qk[2 * s + 1]
                for i, (v, tab) in enumerate(((a, cos_sb), (b, sin_sb), (a, sin_sb), (b, cos_sb))):
                    last = dve.tensor_tensor(rot[4 * s + i][:, :], v[:, :], tab[:, cols], ALU.mult)
            dve_a.mark(last)
            dve_a.settle(dve)
            for s in range(2):
                t = rot[4 * s:4 * s + 4]
                dve.tensor_tensor(qk[2 * s][:, :], t[0][:, :], t[1][:, :], ALU.subtract)
                last = dve.tensor_tensor(qk[2 * s + 1][:, :], t[2][:, :], t[3][:, :], ALU.add)
            dve_a.mark(last)
            dve_a.settle(dve)

        def split(n, th):
            u = 2 * n + th
            need(dve, parts_out, u * PARTS_DMA)
            for i in range(4):
                last = dve.tensor_copy(parts[i // 2][:, 0, i % 2, :], qk[i][:, :])
            dve_a.mark(last)
            dve_a.settle(dve)
            for i in range(4):
                last = dve.tensor_tensor(rot[i][:, :], qk[i][:, :], parts[i // 2][:, 0, i % 2, :], ALU.subtract)
            dve_a.mark(last)
            dve_a.settle(dve)
            for i in range(4):
                last = dve.tensor_copy(parts[i // 2][:, 1, i % 2, :], rot[i][:, :])
            dve_a.mark(last)
            dve_a.settle(dve)
            for i in range(4):
                last = dve.tensor_tensor(parts[i // 2][:, 2, i % 2, :], rot[i][:, :],
                                         parts[i // 2][:, 1, i % 2, :], ALU.subtract)
            last.then_inc(parts_ready, 1)
            dve_a.end()

        def values(n, pair):
            bank = take(n, 18 + pair)
            if pair == 0:
                need(dve, v_ones_ready, NG * n)
            for t in range(2):
                last = dve.tensor_tensor(v_sb[:, 2 * pair + t, :], bank[:, t * D:(t + 1) * D], bv_sb[:, :], ALU.add)
            last.then_inc(side_free, 1)

        def half_job(n, th, k):
            if k < 2:
                turned_x(n, th, k)
            elif k < 4:
                turned_z(n, th, k - 2)
            elif k == 4:
                logits(n, th)
            else:
                biased(n, th, k - 5)

        def copy_o(b, il):
            i = b * 2 * NG + il
            dve.wait_ge(pv_done, (i + 1) * KT)
            need(dve, o_out[il % 2], (b * NG + il // 2) * DMA)
            dve.tensor_copy(o_sb[il % 2][:, :], o_ps[:, :]).then_inc(o_copied, 1)

        def normalise(d):
            dve_d.start(d)
            dve.wait_ge(sums_in, (d + 1) * 8 * DMA)
            dve_d.mark(dve.reciprocal(den[:, :, :], den[:, :, :]))
            dve_d.settle(dve)
            dve_d.mark(dve.tensor_tensor(num[:, :, :], num[:, :, :], den[:, :, :], ALU.mult))
            dve_d.settle(dve)
            dve.wait_ge(base_in, (d + 1) * DMA)

        def quarter_split(d, quarter):
            cols = slice(quarter * 2 * P, (quarter + 1) * 2 * P)
            dve_d.mark(dve.tensor_copy(at_hi[quarter % 2][:, :, :], num[:, :, cols]))
            dve_d.settle(dve)
            dve.tensor_tensor(at_lo[quarter % 2][:, :, :], num[:, :, cols], at_hi[quarter % 2][:, :, :],
                              ALU.subtract).then_inc(at_split, 1)
            if quarter == QUARTERS - 1:
                dve_d.end()

        def add_base(d, quarter):
            dve.wait_ge(wo_done, QUARTERS * d + quarter + 1)
            rows = base[:, 2 * quarter:2 * quarter + 2, :]
            dve.tensor_tensor(rows, wo_ps[:, :, :], rows, ALU.add).then_inc(y_ready, 1)

        def maxima(b, hg):
            u, n = b * NG + hg, HPG * KT
            dve_b.start(u)
            for k in range(n):
                dve.wait_ge(max_full, u * n + k + 1)
                dve.tensor_reduce(row_max[:, k:k + 1], score[k % 2][:, :, :].rearrange("p a n -> p (a n)"),
                                  AX_X, ALU.max).then_inc(max_free, 1)
            dve.wait_ge(max_turned, u + 1)
            need(dve, shift_out, DMA * u)
            dve_b.mark(dve.tensor_scalar(neg_max[:, :], score[0][0:n, 0, 0:P], -1.0, None, ALU.mult))
            dve_b.settle(dve)
            dve_b.mark(dve.tensor_copy(shift[:, 0, :], neg_max[:, :]))
            dve_b.settle(dve)
            dve_b.mark(dve.tensor_tensor(neg_rest[:, :], neg_max[:, :], shift[:, 0, :], ALU.subtract))
            dve_b.settle(dve)
            dve_b.mark(dve.tensor_copy(shift[:, 1, :], neg_rest[:, :]))
            dve_b.settle(dve)
            dve.tensor_tensor(shift[:, 2, :], neg_rest[:, :], shift[:, 1, :], ALU.subtract).then_inc(shift_ready, 1)
            dve_b.end()

        def attend(b, nxt, prev):
            for s in range(STEPS):
                if s % KT == 0:
                    if s > 0:
                        copy_o(b, s // KT - 1)
                    elif prev is not None:
                        copy_o(prev, 2 * NG - 1)
                if s % (2 * KT) == 0:
                    maxima(b, s // (2 * KT))
                if prev is not None:
                    if s == 2:
                        normalise(prev)
                        quarter_split(prev, 0)
                        quarter_split(prev, 1)
                    if s in WO_STEP:
                        quarter = WO_STEP.index(s)
                        add_base(prev, quarter)
                        if quarter + 2 < QUARTERS:
                            quarter_split(prev, quarter + 2)
                if nxt is not None:
                    for th, at in ((0, 8), (1, 24)):
                        if s == at + (th == 0):
                            norm1(nxt, th)
                        if s == at + 2:
                            norm2(nxt, th)
                        if s == at + 4:
                            norm3(nxt, th)
                        for k in range(9):
                            if HALF_STEPS[th][k] == s:
                                half_job(nxt, th, k)
                        if s == HALF_STEPS[th][-1] + 1:
                            affinities(nxt, th)
                            rotary(nxt, th)
                        if s == HALF_STEPS[th][-1] + 4:
                            split(nxt, th)
                    if s in V_STEP:
                        values(nxt, V_STEP.index(s))

        for i in range(2):
            dve.memset(k_stack[i][SHIFT:FULL, :, :], 1.0).then_inc(ones_set, 1)
        dve.wait_ge(weights_in, 4 * DMA)
        raw = [probs[0][:, i, :].rearrange("p (c n) -> p c n", c=DC) for i in range(4)]
        for i in range(4):
            last = dve.tensor_copy(w_hi[i][:, :, :], raw[i])
        last.then_inc(weights_high, 1)
        dve.wait_ge(weights_high, 1)
        for i in range(4):
            last = dve.tensor_tensor(w_lo[i][:, :, :], raw[i], w_hi[i][:, :, :], ALU.subtract)
        last.then_inc(weights_split, 1)
        dve.wait_ge(const_in, CONSTS * DMA)
        for th in range(2):
            norm1(0, th)
            norm2(0, th)
            norm3(0, th)
            for k in range(9):
                half_job(0, th, k)
            affinities(0, th)
            rotary(0, th)
            split(0, th)
        for pair in range(4):
            values(0, pair)
        attend(0, 1, None)
        with dve.Fori(1, NB - 1) as b:
            attend(b, b + 1, b - 1)
        attend(NB - 1, None, NB - 2)
        copy_o(NB - 1, 2 * NG - 1)
        normalise(NB - 1)
        quarter_split(NB - 1, 0)
        quarter_split(NB - 1, 1)
        for quarter in range(QUARTERS):
            add_base(NB - 1, quarter)
            if quarter + 2 < QUARTERS:
                quarter_split(NB - 1, quarter + 2)
        dve.wait_ge(aff_turned, 1)
        for half in range(2):
            last = dve.tensor_copy(top_scores[:, half * HALF:(half + 1) * HALF]
                                   .rearrange("p (a n) -> p a n", a=2), score[half][0:BE, :, 0:2 * P])
        last.then_inc(top_copied, 1)
        dve.wait_ge(top_copied, 1)
        dve_t.start(0)
        for r in range(CAP // 8):
            eight = slice(8 * r, 8 * r + 8)
            dve_t.mark(dve.max(top_gate[:, eight], top_scores))
            dve_t.settle(dve)
            dve_t.mark(dve.max_index(top_row[:, eight], top_gate[:, eight], top_scores))
            dve_t.settle(dve)
            dve_t.mark(dve.match_replace(top_scores, top_gate[:, eight], top_scores, -1.0))
            dve_t.settle(dve)


def expert_part(nc, ctx, g):
    (T, D, NB, S, DC, E, CAP, BE, F, FC) = (g[k] for k in "T D NB S DC E CAP BE F FC".split())
    out, xn_dram, wg, wu, wd = (g[k] for k in "out xn_dram wg wu wd".split())
    ident_sb, row0_sb, top_gate, top_row = (g[k] for k in "ident_sb row0_sb top_gate top_row".split())
    SLOTS = 4 * P
    ST = SLOTS // P
    HALVES = CAP // P
    UNITS = NB * HALVES // ST
    COLS = NB * HALVES

    def sb(name, shape, dt=F32):
        return ctx.enter_context(nc.sbuf_tensor(name, shape, dt))

    def ps(name, shape):
        return ctx.enter_context(nc.psum_tensor(name, shape, F32))

    def sem(name):
        return ctx.enter_context(nc.semaphore(name))

    row_f = sb("row_f", [BE, CAP])
    rows_all = sb("rows_all", [P, E, NB, HALVES], U32)
    gates_all = sb("gates_all", [P, E, NB, HALVES])
    rows_flat = rows_all[:, :, :, :].rearrange("p e b h -> p (e b h)")
    gates_flat = gates_all[:, :, :, :].rearrange("p e b h -> p (e b h)")
    rows_now = [sb(f"rows_now{i}", [P, ST], U32) for i in range(UNITS)]
    shapes = ([P, DC, F], [P, DC, F], [P, FC, D])
    w_raw = [sb(f"w_raw{i}", s) for i, s in enumerate(shapes)]
    w_hi = [[sb(f"we_hi{k}{i}", s, F32R) for i, s in enumerate(shapes)] for k in range(2)]
    w_lo = [[sb(f"we_lo{k}{i}", s, F32R) for i, s in enumerate(shapes)] for k in range(2)]
    GATE, UP, DOWN = range(3)
    xs = [sb(f"xs{i}", [P, ST, D]) for i in range(2)]
    x_hi, x_lo = sb("x_hi", [P, DC, SLOTS], F32R), sb("x_lo", [P, DC, SLOTS], F32R)
    silu = [sb(f"silu{i}", [P, SLOTS]) for i in range(2)]
    h = [sb(f"h{i}", [P, SLOTS]) for i in range(2)]
    h_hi, h_lo = sb("h_hi", [P, FC, SLOTS], F32R), sb("h_lo", [P, FC, SLOTS], F32R)
    y = [[sb(f"y{i}{t}", [P, D]) for t in range(ST)] for i in range(2)]

    g_ps = [ps(f"g_ps{i}", [P, SLOTS]) for i in range(2)]
    u_ps = [ps(f"u_ps{i}", [P, SLOTS]) for i in range(2)]
    xt_ps = [ps(f"xt_ps{i}", [P, SLOTS]) for i in range(DC)]
    d_ps = [ps(f"d_ps{i}", [P, SLOTS]) for i in range(2)]

    row_cast, row_added, top_turned, top_spread = (
        sem(n) for n in ("row_cast", "row_added", "top_turned", "top_spread"))
    w_in, w_high, w_split = sem("w_in"), sem("w_high"), sem("w_split")
    rows_set = sem("rows_set")
    gathered = [sem(f"gathered{i}") for i in range(2)]
    scattered = [sem(f"scattered{i}") for i in range(UNITS)]
    xt_full, x_high, x_split = sem("xt_full"), sem("x_high"), sem("x_split")
    gu_full, silu_done, h_done, h_high, h_split = (
        sem(n) for n in ("gu_full", "silu_done", "h_done", "h_high", "h_split"))
    down_full, y_scaled = sem("down_full"), sem("y_scaled")
    passed = sem("passed_e")

    def need(eng, s, value):
        if not isinstance(value, int) or value > 0:
            eng.wait_ge(s, value)

    def hold(eng, s, value):
        need(eng, s, value)
        if not isinstance(value, int):
            eng.sem_inc(passed, 1)

    def experts(eng, pair):
        pair(0, False)
        with eng.Fori(1, E // 2 - 1) as p:
            pair(p, False)
        pair(E // 2 - 1, True)

    block = ctx.enter_context(nc.Block())

    @block.sync
    def _(sp):
        def load(e):
            for raw, dram in zip(w_raw, (wg, wu, wd)):
                sp.dma_start(raw[:, :, :], dram[e].rearrange("(c p) n -> p c n", p=P)).then_inc(w_in, DMA)

        def pair(p, last):
            for k in range(2):
                if not (last and k == 1):
                    hold(sp, w_split, 2 * p + k + 1)
                    load(2 * p + k + 1)

        load(0)
        experts(sp, pair)

    @block.gpsimd
    def _(pool):
        def gather(e, bp, par):
            unit = UNITS * e + bp
            need(pool, scattered[bp], ST * DMA * e)
            hold(pool, xt_full, DC * (unit - 1))
            pool.tensor_copy(rows_now[bp][:, :], rows_flat[:, bass.ds(e * COLS + bp * ST, ST)]).then_inc(rows_set, 1)
            hold(pool, rows_set, unit + 1)
            for t in range(ST):
                pool.indirect_dma_start(xs[par][:, t, :], None, xn_dram[:, :],
                                        bass.IndirectOffsetOnAxis(ap=rows_now[bp][:, t:t + 1], axis=0))\
                    .then_inc(gathered[par], DMA)

        def scatter(e, bp, par):
            unit = UNITS * e + bp
            for t in range(ST):
                hold(pool, y_scaled, ST * unit + t + 1)
                pool.indirect_dma_start(out[:, :], bass.IndirectOffsetOnAxis(ap=rows_now[bp][:, t:t + 1], axis=0),
                                        y[par][t][:, :], None, compute_op=ALU.add)\
                    .then_inc(scattered[bp], DMA)

        def pair(p, last):
            for k in range(2):
                for bp in range(UNITS):
                    e, n = 2 * p + k, k * UNITS + bp
                    if not (last and n == 2 * UNITS - 1):
                        gather(e + (bp + 1) // UNITS, (bp + 1) % UNITS, (n + 1) % 2)
                    scatter(e, bp, n % 2)

        pool.wait_ge(top_spread, 2 * HALVES)
        gather(0, 0, 0)
        experts(pool, pair)
        for bp in range(UNITS):
            pool.wait_ge(scattered[bp], ST * DMA * E)

    @block.scalar
    def _(act):
        def split_w(e, k):
            act.wait_ge(w_in, 3 * DMA * (e + 1))
            for raw, hi in zip(w_raw, w_hi[k]):
                last = act.copy(hi[:, :, :], raw[:, :, :])
            last.then_inc(w_high, 1)

        def turned(unit):
            for c in range(DC):
                act.wait_ge(xt_full, DC * unit + c + 1)
                act.copy(x_hi[:, c, :], xt_ps[c][:, :]).then_inc(x_high, 1)

        def high(unit, f):
            act.wait_ge(h_done, FC * unit + f + 1)
            act.copy(h_hi[:, f, :], h[f % 2][:, :]).then_inc(h_high, 1)

        def pair(p, last):
            for k in range(2):
                for bp in range(UNITS):
                    unit = UNITS * (2 * p + k) + bp
                    for f in range(FC):
                        act.wait_ge(gu_full, FC * unit + f + 1)
                        act.activation(silu[f % 2][:, :], g_ps[f % 2][:, :], ACT.Silu).then_inc(silu_done, 1)
                        if f > 0:
                            high(unit, f - 1)
                    high(unit, FC - 1)
                    if not (last and k == 1):
                        if bp == 1:
                            split_w(2 * p + k + 1, 1 - k)
                    if not (last and k == 1 and bp == UNITS - 1):
                        turned(unit + 1)

        split_w(0, 0)
        turned(0)
        experts(act, pair)

    @block.tensor
    def _(pe):
        def turn(unit, par):
            pe.wait_ge(gathered[par], ST * DMA * ((unit - par) // 2 + 1) if isinstance(unit, int)
                       else (unit - par) * (ST * DMA // 2) + ST * DMA)
            for c in range(DC):
                need(pe, x_split, DC * unit + c - 1)
                for t in range(ST):
                    last = pe.transpose(xt_ps[c][:, t * P:(t + 1) * P], xs[par][:, t, c * P:(c + 1) * P], ident_sb[:, :])
                last.then_inc(xt_full, 1)

        def gate_up(unit, k):
            pe.wait_ge(x_split, DC * unit + DC)
            for f in range(FC):
                need(pe, h_done, FC * unit + f - 1)
                for w, bank in ((GATE, g_ps), (UP, u_ps)):
                    for i, (wt, xt) in enumerate(((w_hi, x_hi), (w_lo, x_hi), (w_hi, x_lo))):
                        for c in range(DC):
                            last = pe.matmul(bank[f % 2][:, :], wt[k][w][:, c, f * P:(f + 1) * P], xt[:, c, :],
                                             start=i == 0 and c == 0, stop=i == 2 and c == DC - 1)
                last.then_inc(gu_full, 1)

        def down(unit, k):
            def part(t, fs):
                for f in fs:
                    pe.wait_ge(h_split, FC * unit + f + 1)
                    for i, (ht, wt) in enumerate(((h_hi, w_hi), (h_lo, w_hi), (h_hi, w_lo))):
                        last = pe.matmul(d_ps[t % 2][:, 0:D], ht[:, f, t * P:(t + 1) * P], wt[k][DOWN][:, f, :],
                                         start=i == 0 and f == 0, stop=i == 2 and f == FC - 1)
                return last

            for t in range(2):
                need(pe, y_scaled, ST * unit + t - 1)
                part(t, range(FC - 1))
            for t in range(2):
                part(t, (FC - 1,)).then_inc(down_full, 1)
            for t in range(2, ST):
                pe.wait_ge(y_scaled, ST * unit + t - 1)
                part(t, range(FC)).then_inc(down_full, 1)

        def pair(p, last):
            for k in range(2):
                for bp in range(UNITS):
                    e, n = 2 * p + k, k * UNITS + bp
                    unit = UNITS * e + bp
                    if bp == 0:
                        pe.wait_ge(w_split, e + 1)
                    gate_up(unit, k)
                    if not (last and n == 2 * UNITS - 1):
                        turn(unit + 1, (n + 1) % 2)
                    down(unit, k)

        pe.wait_ge(row_added, 1)
        for i, src in enumerate((row_f, top_gate)):
            for half in range(HALVES):
                last = pe.transpose(d_ps[i][:, half * BE:(half + 1) * BE], src[:, half * P:(half + 1) * P],
                                    ident_sb[0:BE, 0:BE])
        last.then_inc(top_turned, 1)
        turn(0, 0)
        experts(pe, pair)

    @block.vector
    def _(dve):
        def split_w(e, k):
            dve.wait_ge(w_high, e + 1)
            for raw, hi, lo in zip(w_raw, w_hi[k], w_lo[k]):
                last = dve.tensor_tensor(lo[:, :, :], raw[:, :, :], hi[:, :, :], ALU.subtract)
            last.then_inc(w_split, 1)

        def turned(unit):
            for c in range(DC):
                dve.wait_ge(x_high, DC * unit + c + 1)
                dve.tensor_tensor(x_lo[:, c, :], xt_ps[c][:, :], x_hi[:, c, :], ALU.subtract).then_inc(x_split, 1)

        def low(unit, f):
            dve.wait_ge(h_high, FC * unit + f + 1)
            dve.tensor_tensor(h_lo[:, f, :], h[f % 2][:, :], h_hi[:, f, :], ALU.subtract).then_inc(h_split, 1)

        def pair(p, last):
            for k in range(2):
                for bp in range(UNITS):
                    e, n = 2 * p + k, k * UNITS + bp
                    unit = UNITS * e + bp
                    for f in range(FC):
                        dve.wait_ge(silu_done, FC * unit + f + 1)
                        need(dve, h_split, FC * unit + f - 1)
                        dve.tensor_tensor(h[f % 2][:, :], u_ps[f % 2][:, :], silu[f % 2][:, :], ALU.mult)\
                           .then_inc(h_done, 1)
                        if f > 0:
                            low(unit, f - 1)
                    low(unit, FC - 1)
                    if bp == 1 and not (last and k == 1):
                        split_w(e + 1, 1 - k)
                    if not (last and n == 2 * UNITS - 1):
                        turned(unit + 1)
                    need(dve, scattered[(bp - 2) % UNITS], ST * DMA * (e + (bp >= 2)))
                    for t in range(ST):
                        dve.wait_ge(down_full, ST * unit + t + 1)
                        dve.tensor_scalar(y[n % 2][t][:, :], d_ps[t % 2][:, 0:D],
                                          gates_flat[:, bass.ds(e * COLS + bp * ST + t, 1)], None, ALU.mult)\
                           .then_inc(y_scaled, 1)

        dve.tensor_copy(row_f[:, :], top_row[:, :]).then_inc(row_cast, 1)
        dve.wait_ge(row_cast, 1)
        dve.tensor_scalar(row_f[:, :], row_f[:, :], row0_sb[:, :], None, ALU.add).then_inc(row_added, 1)
        dve.wait_ge(top_turned, 1)
        for i, to in enumerate((rows_all, gates_all)):
            for half in range(HALVES):
                dve.tensor_copy(to[:, :, :, half], d_ps[i][:, half * BE:(half + 1) * BE]
                                .rearrange("p (b e) -> p e b", e=E)).then_inc(top_spread, 1)
        dve.wait_ge(top_spread, 2 * HALVES)
        split_w(0, 0)
        turned(0)
        experts(dve, pair)


def kernel(**inputs):
    import numpy as np
    import concourse.bacc as bacc
    from concourse.bass_utils import run_bass_kernel_spmd as run

    x = np.ascontiguousarray(inputs["L0_attn_x"])
    NB, S, D = x.shape
    HD = D // NHEAD
    order = np.arange(D).reshape(NHEAD, HD // 2, 2).transpose(2, 0, 1).reshape(D)
    inv_freq = np.float32(1.0) / np.float32(10000.0) ** (np.arange(0, HD, 2, dtype=np.float32) / np.float32(HD))
    angle = np.outer(np.arange(S, dtype=np.float32), inv_freq).astype(np.float32)

    def columns(v):
        return v.reshape(-1, P).T

    arrays = {
        "x": x.reshape(NB * S, D),
        "ln_w": columns(inputs["L0_attn_ln_w"]), "ln_b": columns(inputs["L0_attn_ln_b"]),
        "wq_t": inputs["L0_attn_Wq"].T[:, order], "wk_t": inputs["L0_attn_Wk"].T[:, order],
        "wv_t": inputs["L0_attn_Wv"].T, "wo_t": inputs["L0_attn_Wo"].T,
        "bq": columns(inputs["L0_attn_bq"][order]), "bk": columns(inputs["L0_attn_bk"][order]),
        "bv": inputs["L0_attn_bv"], "bo": inputs["L0_attn_bo"],
        "gate_w": inputs["L0_ffn_gate_w"],
        "wg": inputs["L0_ffn_Wg"], "wu": inputs["L0_ffn_Wu"], "wd": inputs["L0_ffn_Wd"],
        "cos": np.tile(np.cos(angle).T, (NHEAD, 1)), "sin": np.tile(np.sin(angle).T, (NHEAD, 1)),
        "ident": np.eye(P, dtype=np.float32),
        "row0": np.repeat(np.arange(NB, dtype=np.float32) * S, NEXPERT)[:, None],
    }
    arrays = {k: np.ascontiguousarray(v) for k, v in arrays.items()}
    nc = bacc.Bacc("TRN2", target_bir_lowering=False, num_devices=1)
    args = {k: nc.dram_tensor(f"in_{k}", v.shape, mybir.dt.from_np(v.dtype), kind="ExternalInput").ap()
            for k, v in arrays.items()}
    out = nc.dram_tensor("out_0", (NB * S, D), F32, kind="ExternalOutput").ap()
    build(nc, **args, out=out)
    r = run(nc, [{f"in_{k}": v for k, v in arrays.items()}], core_ids=[0])
    return r.results[0]["out_0"].reshape(NB, S, D)
```

```python
from contextlib import ExitStack

import concourse.bass as bass
import numpy as np
from concourse import mybir

ACT = mybir.ActivationFunctionType
ALU = mybir.AluOpType
AX_X = mybir.AxisListType.X
F32 = mybir.dt.float32
F32R = mybir.dt.float32r
BF16 = mybir.dt.bfloat16
U32 = mybir.dt.uint32

P = 128
LN_EPS = 1e-5
NHEAD = 16
NEXPERT = 8
DMA = 16
HPG = 4
KEYS_W = 32
NPART = 3

Q_PARTS = (0, 0, 1, 1, 0, 2)
K_PARTS = (0, 1, 0, 1, 2, 0)


SCORE_LIMIT = 78.0
VALUE_LIMIT = 32.0


class Tally:

    def __init__(self, sem, per):
        self.sem, self.per, self.base, self.count = sem, per, 0, 0

    def start(self, n):
        self.base, self.count = n * self.per, 0

    def mark(self, instruction):
        instruction.then_inc(self.sem, 1)
        self.count += 1
        assert self.count <= self.per

    def settle(self, eng, wait=None):
        if wait:
            wait(eng, self.sem, self.base + self.count)
        else:
            eng.wait_ge(self.sem, self.base + self.count)

    def end(self):
        assert self.count == self.per, (self.count, self.per)


def build(nc, x, ln_w, ln_b, wq_t, wk_t, wv_t, wo_t, bq, bk, bv, bo, gate_w, wg, wu, wd,
          cos, sin, ident, row0, heads, out):
    T, D = x.shape
    NB = 8
    S = T // NB
    TT = S // P
    DC = D // P
    HALF = S // 2
    HT = HALF // P
    HD = D // NHEAD
    HR = HD // 2
    NG = NHEAD // HPG
    KT = S // P
    STEPS = NG * 2 * KT
    ROWS = len(Q_PARTS) * HD
    SHIFT = ROWS
    FULL = ROWS + NPART
    SCALE = float(HD) ** -0.5
    E = NEXPERT
    CAP = 2 * S // E
    BE = NB * E
    F = wg.shape[2]
    FC = F // P

    q_dram = nc.dram_tensor("q_parts", (NB, NPART, NHEAD, 2, HR, S), BF16).ap()
    k_dram = nc.dram_tensor("k_parts", (NB, NPART, NHEAD, 2, HR, S), BF16).ap()
    shift_dram = nc.dram_tensor("shift_parts", (NB, NG, NPART, HPG * KT, P), BF16).ap()
    o_dram = nc.dram_tensor("o_sums", (NB, 2, NG, HPG, 2, HD, HALF), F32).ap()
    rec_dram = nc.dram_tensor("den_recs", (NB, 2, NHEAD, HALF), F32).ap()
    xn_dram = nc.dram_tensor("xn_rows", (T, D), F32).ap()

    outer = ExitStack()
    with outer:
        def sem(name):
            return outer.enter_context(nc.semaphore(name))

        def keep(name, shape, dt):
            return outer.enter_context(nc.sbuf_tensor(name, shape, dt))

        ident_sb = keep("ident_sb", [P, P], F32)
        row0_sb = keep("row0_sb", [BE, 1], F32)
        affinity = keep("affinity", [P, TT, BE], F32)
        top_gate = keep("top_gate", [BE, CAP], F32)
        top_row = keep("top_row", [BE, CAP], U32)

        with ExitStack() as inner:
            attention_part(nc, inner, locals())
        with ExitStack() as inner:
            expert_part(nc, inner, locals())


def attention_part(nc, ctx, g):
    (T, D, NB, S, TT, DC, HALF, HT, HD, HR, NG, KT, STEPS, ROWS, SHIFT, FULL, SCALE, E, CAP, BE) = (
        g[k] for k in "T D NB S TT DC HALF HT HD HR NG KT STEPS ROWS SHIFT FULL SCALE E CAP BE".split())
    x, out, q_dram, k_dram, shift_dram, o_dram, rec_dram, xn_dram = (
        g[k] for k in "x out q_dram k_dram shift_dram o_dram rec_dram xn_dram".split())
    ident_sb, row0_sb, affinity, top_gate, top_row = (
        g[k] for k in "ident_sb row0_sb affinity top_gate top_row".split())

    def sb(name, shape, dt=F32):
        return ctx.enter_context(nc.sbuf_tensor(name, shape, dt))

    def ps(name, shape):
        return ctx.enter_context(nc.psum_tensor(name, shape, F32))

    def sem(name):
        return ctx.enter_context(nc.semaphore(name))

    w_hi = [sb(f"w_hi{i}", [P, DC, D], F32R) for i in range(4)]
    w_lo = [sb(f"w_lo{i}", [P, DC, D], F32R) for i in range(4)]
    WQ, WK, WV, WO = range(4)
    cos_sb, sin_sb = sb("cos_sb", [P, S]), sb("sin_sb", [P, S])
    gate_sb = sb("gate_sb", [P, DC, E])
    lnw_sb, lnb_sb = sb("lnw_sb", [P, DC]), sb("lnb_sb", [P, DC])
    bq_sb, bk_sb = sb("bq_sb", [P, 2]), sb("bk_sb", [P, 2])
    bv_sb, bo_sb = sb("bv_sb", [P, D]), sb("bo_sb", [P, D])
    minus_half = sb("minus_half", [P, HT])
    heads_sb = sb("heads_sb", [P, KEYS_W])
    peaks = sb("peaks", [P, 4])
    norms = sb("norms", [1, P])
    terms = sb("terms", [1, KEYS_W + 2 * P + 1])
    bound = sb("bound", [1, NB])
    xin, xn, z = (sb(n, [P, HT, D]) for n in ("xin", "xn", "z"))
    stats = sb("stats", [P, HT, 6])
    mv1, mv2 = sb("mv1", [P, HT, 2]), sb("mv2", [P, HT, 2])
    ve1, ve2 = sb("ve1", [P, HT]), sb("ve2", [P, HT])
    rstd1, rstd2 = sb("rstd1", [P, HT]), sb("rstd2", [P, HT])
    xnT = sb("xnT", [P, DC, HALF])
    znT = sb("znT", [P, DC, HALF])
    zn_hi, zn_lo = sb("zn_hi", [P, DC, S], F32R), sb("zn_lo", [P, DC, S], F32R)
    lg_max, lg_sum, lg_rec = (sb(n, [P, HT]) for n in ("lg_max", "lg_sum", "lg_rec"))
    lg, lg_exp = sb("lg", [P, HT, E]), sb("lg_exp", [P, HT, E])
    qk = [sb(f"qk{i}", [P, HALF]) for i in range(4)]
    rot = [sb(f"rot{i}", [P, HALF]) for i in range(8)]
    parts = [sb(f"parts{i}", [P, NPART, 2, HALF], BF16) for i in range(2)]
    v_sb = sb("v_sb", [P, KT, D])
    q_stack = [sb(f"q_stack{i}", [P, HPG, S], BF16) for i in range(2)]
    k_stack = [sb(f"k_stack{i}", [P, HPG, S], BF16) for i in range(2)]
    v_ones = [sb(f"v_ones{i}", [P, KT, HPG, KEYS_W]) for i in range(2)]
    probs = [sb(f"probs{i}", [P, HPG, HALF]) for i in range(2)]
    row_max = sb("row_max", [P, HPG * KT])
    neg_max, neg_rest = sb("neg_max", [HPG * KT, P]), sb("neg_rest", [HPG * KT, P])
    shift = sb("shift", [HPG * KT, NPART, P], BF16)
    o_sb = [sb(f"o_sb{i}", [P, HALF]) for i in range(2)]
    num, rec = sb("num", [P, DC, S]), sb("rec", [P, DC, S])
    at_hi = [sb(f"at_hi{i}", [P, DC, 2 * P], F32R) for i in range(2)]
    at_lo = [sb(f"at_lo{i}", [P, DC, 2 * P], F32R) for i in range(2)]
    base = sb("base", [P, TT, D])
    den, den_rec = (xnT[0:2 * NHEAD, i, :] for i in range(2))
    top_scores = znT[0:BE, :, :].rearrange("p c n -> p (c n)")

    score = [ps(f"score{i}", [P, 2, HALF]) for i in range(2)]
    o_ps = ps("o_ps", [P, HALF])
    wo_ps = ps("wo_ps", [P, 2, D])
    side = [ps(f"side{i}", [P, HALF]) for i in range(2)]

    const_in, weights_in = sem("const_in"), sem("weights_in")
    ones_set, zeros_set, passed = sem("ones_set"), sem("zeros_set"), sem("passed")
    const_set, weights_split, weights_high = sem("const_set"), sem("weights_split"), sem("weights_high")
    x_in, base_out, xn_out = sem("x_in"), sem("base_out"), sem("xn_out")
    stats1_done, stats2_done, rstd1_done, rstd2_done = (
        sem(n) for n in ("stats1_done", "stats2_done", "rstd1_done", "rstd2_done"))
    xn_ready, z_ready = sem("xn_ready"), sem("z_ready")
    side_full, side_free = sem("side_full"), sem("side_free")
    zn_ready, lg_exped, aff_done = sem("zn_ready"), sem("lg_exped"), sem("aff_done")
    parts_ready, parts_out = sem("parts_ready"), sem("parts_out")
    v_ones_ready = sem("v_ones_ready")
    stack_in = [sem(f"stack_in{i}") for i in range(2)]
    max_full, max_free, max_turned = sem("max_full"), sem("max_free"), sem("max_turned")
    shift_ready, shift_out, shift_in = sem("shift_ready"), sem("shift_out"), sem("shift_in")
    qk_done = [sem(f"qk_done{i}") for i in range(2)]
    exp_done = [sem(f"exp_done{i}") for i in range(2)]
    pv_done, o_copied = sem("pv_done"), sem("o_copied")
    o_out = [sem(f"o_out{i}") for i in range(2)]
    den_in, den_done, rec_out = sem("den_in"), sem("den_done"), sem("rec_out")
    sums_in, base_in, y_out = sem("sums_in"), sem("base_in"), sem("y_out")
    at_split, wo_done, y_ready = sem("at_split"), sem("wo_done"), sem("y_ready")
    aff_turned, top_copied = sem("aff_turned"), sem("top_copied")
    dve_a = Tally(sem("dve_a"), 16)
    dve_b = Tally(sem("dve_b"), 4)
    dve_f = Tally(sem("dve_f"), 3)
    rotated, divided, sq_ready, v_peaked, bound_ready = (sem(n) for n in ("rotated", "divided", "sq_ready", "v_peaked", "bound_ready"))
    dve_d = Tally(sem("dve_d"), 4)
    dve_t = Tally(sem("dve_t"), 3 * CAP // 8)
    pool_a = Tally(sem("pool_a"), 4)

    HPC = P // HD
    CONSTS = 12
    HJOBS = 10
    VJOB = 2 * HJOBS
    PJOB = VJOB + 4
    JOBS = PJOB + 2
    LIMIT = (SCORE_LIMIT / SCALE) ** 2
    LIMIT_BITS = int(np.float32(LIMIT).view(np.int32))
    QUARTERS = S // (2 * P)
    PARTS_DMA = 2 * NPART * 2 * DMA

    ROUTER_STEP = (16, 37)
    DEN_STEP, SUMS_STEP = 6, 28
    WO_STEP = (30, 31, 34, 35)
    HALF_STEPS = ((12, 13, 13, 14, 15, 17, 18, 19, 20, 28), (32, 33, 34, 35, 36, 38, 39, 40, 41, 48))
    V_STEP = (49, 51, 53, 55)
    NORM_STEP = (8, 27)
    TOP_OPS = 3 * CAP // 8
    PEAK_STEP = (58, 59)
    PARTS_STEP = (HALF_STEPS[0][8] + 1, HALF_STEPS[1][8] + 1)

    def need(eng, s, value):
        if not isinstance(value, int) or value > 0:
            eng.wait_ge(s, value)

    def hold(eng, s, value):
        need(eng, s, value)
        if not isinstance(value, int):
            eng.sem_inc(passed, 1)

    def scores_wide(eng, b):
        hold(eng, bound_ready, b + 1)
        bits = bound[0:1, b:b + 1] if isinstance(b, int) else bound[0:1, bass.ds(b, 1)]
        return eng.value_load(bits.bitcast(mybir.dt.int32), min_val=0, max_val=2 ** 31 - 1) > LIMIT_BITS

    def passes_on(eng, *counts):
        for s, n in counts:
            eng.sem_inc(s, n)

    block = ctx.enter_context(nc.Block())

    @block.sync
    def _(sp):
        consts = ((ident_sb[:, :], g["ident"]), (row0_sb[:, :], g["row0"]),
                  (cos_sb[:, :], g["cos"]), (sin_sb[:, :], g["sin"]),
                  (gate_sb[:, :, :], g["gate_w"].rearrange("(c p) e -> p c e", p=P)),
                  (heads_sb[:, :], g["heads"]),
                  (lnw_sb[:, :], g["ln_w"]),
                  (lnb_sb[:, :], g["ln_b"]),
                  (bq_sb[:, :], g["bq"]),
                  (bk_sb[:, :], g["bk"]),
                  (bv_sb[:, :], g["bv"].partition_broadcast(P)),
                  (bo_sb[:, :], g["bo"].partition_broadcast(P)))
        assert len(consts) == CONSTS
        for i, name in enumerate(("wq_t", "wk_t", "wv_t", "wo_t")):
            sp.dma_start(probs[0][:, i, :].rearrange("p (c n) -> p c n", c=DC),
                         g[name].rearrange("(c p) n -> p c n", p=P)).then_inc(weights_in, DMA)
        for to, of in consts:
            sp.dma_start(to, of).then_inc(const_in, DMA)

        def load_stack(b, hg):
            par = hg % 2
            for r, (qp, kp) in enumerate(zip(Q_PARTS, K_PARTS)):
                for stack, dram, part in ((q_stack[par], q_dram, qp), (k_stack[par], k_dram, kp)):
                    sp.dma_start(stack[r * HD:(r + 1) * HD, :, :],
                                 dram[b, part, hg * HPG:(hg + 1) * HPG].rearrange("h a i n -> (a i) h n"))\
                      .then_inc(stack_in[par], DMA)

        def store_parts(n, th):
            hold(sp, parts_ready, 2 * n + th + 1)
            for src, dram in ((0, q_dram), (1, k_dram)):
                for part in range(NPART):
                    for a in range(2):
                        sp.dma_start(dram[n, part, :, a, :, th * HALF:(th + 1) * HALF],
                                     parts[src][:, part, a, :]).then_inc(parts_out, DMA)

        def shift_rows(b, hg, wide):
            u = b * NG + hg
            with sp.If(wide):
                hold(sp, shift_ready, u + 1)
                sp.dma_start(shift_dram[b, hg].rearrange("c t n -> t c n"), shift[:, :, :])\
                  .then_inc(shift_out, DMA)
                hold(sp, shift_out, DMA * (u + 1))
                sp.dma_start(q_stack[hg % 2][SHIFT:FULL, :, :].rearrange("c h n -> c (h n)"),
                             shift_dram[b, hg].rearrange("c t n -> c (t n)")).then_inc(shift_in, DMA)
            with sp.Else():
                passes_on(sp, (shift_out, DMA), (shift_in, DMA))

        def store_o(b, il):
            i = b * 2 * NG + il
            hold(sp, o_copied, i + 1)
            sp.dma_start(o_dram[b, il % 2, il // 2].rearrange("j w r n -> (j w r) n"),
                         o_sb[il % 2][:, :]).then_inc(o_out[il % 2], DMA)

        def load_sums(d):
            for i in range(2):
                hold(sp, o_out[i], DMA * NG * (d + 1))
            sp.dma_start(den, o_dram[d, :, :, :, 1, 0, :].rearrange("q g j n -> (q g j) n")).then_inc(den_in, DMA)
            for qh in range(2):
                for c in range(DC):
                    src = o_dram[d, qh, 2 * c:2 * c + 2].rearrange("g j w r n -> w (g j) r n")
                    sp.dma_start(num[:, c, qh * HALF:(qh + 1) * HALF], src[0]).then_inc(sums_in, DMA)
            hold(sp, base_out, 2 * DMA * (d + 1))
            rows = out[bass.ds(d * S, S), :].rearrange("(t p) n -> p t n", p=P)
            sp.dma_start(base[:, :, :], rows).then_inc(base_in, DMA)

        def spread_rec(d):
            hold(sp, den_done, d + 1)
            sp.dma_start(rec_dram[d].rearrange("q h n -> (q h) n"), den_rec).then_inc(rec_out, DMA)
            hold(sp, rec_out, DMA * (d + 1))
            for qh in range(2):
                for c in range(DC):
                    src = rec_dram[d, qh, c * HPC:(c + 1) * HPC].unsqueeze(1).to_broadcast([HPC, HD, HALF])
                    sp.dma_start(rec[:, c, qh * HALF:(qh + 1) * HALF], src).then_inc(sums_in, DMA)

        def store_y(d):
            rows = out[bass.ds(d * S, S), :].rearrange("(t p) n -> p t n", p=P)
            for hf in range(2):
                hold(sp, y_ready, QUARTERS * d + 2 * hf + 2)
                sp.dma_start(rows[:, hf * HT:(hf + 1) * HT, :], base[:, hf * HT:(hf + 1) * HT, :])\
                  .then_inc(y_out, DMA)

        def first_stack(n):
            hold(sp, parts_out, (n + 1) * 2 * PARTS_DMA)
            load_stack(n, 0)

        def attend(b, nxt, prev):
            wide = scores_wide(sp, b)
            hold(sp, exp_done[1], b * STEPS)
            load_stack(b, 1)
            shift_rows(b, 0, wide)
            if prev is not None:
                store_o(prev, 2 * NG - 1)
                load_sums(prev)
                spread_rec(prev)
            store_o(b, 0)
            hold(sp, exp_done[1], b * STEPS + 2 * KT)
            shift_rows(b, 1, wide)
            load_stack(b, 2)
            store_o(b, 1)
            store_o(b, 2)
            if nxt is not None:
                store_parts(nxt, 0)
            hold(sp, exp_done[1], b * STEPS + 4 * KT)
            shift_rows(b, 2, wide)
            load_stack(b, 3)
            store_o(b, 3)
            if prev is not None:
                store_y(prev)
                hold(sp, y_out, 2 * DMA * (prev + 1))
            store_o(b, 4)
            hold(sp, exp_done[1], b * STEPS + 6 * KT)
            shift_rows(b, 3, wide)
            store_o(b, 5)
            if nxt is not None:
                store_parts(nxt, 1)
                first_stack(nxt)
            store_o(b, 6)

        store_parts(0, 0)
        store_parts(0, 1)
        first_stack(0)
        attend(0, 1, None)
        with sp.Fori(1, NB - 1) as b:
            attend(b, b + 1, b - 1)
        attend(NB - 1, None, NB - 2)
        store_o(NB - 1, 2 * NG - 1)
        load_sums(NB - 1)
        spread_rec(NB - 1)
        store_y(NB - 1)
        hold(sp, y_out, 2 * DMA * NB)

    @block.gpsimd
    def _(pool):
        pool.memset(minus_half[:, :], -0.5).then_inc(const_set, 1)
        for i in range(2):
            pool.memset(v_ones[i][:, :, :, :], 1.0).then_inc(const_set, 1)

        def norm(n, th):
            u = 2 * n + th
            pool_a.start(u)
            hold(pool, base_out, DMA * u)
            pool.dma_start(xin[:, :, :], x[bass.ds(n * S + th * HALF, HALF), :]
                           .rearrange("(t p) n -> p t n", p=P)).then_inc(x_in, DMA)
            for stats_done, mv, ve, rstd, rstd_done in ((stats1_done, mv1, ve1, rstd1, rstd1_done),
                                                        (stats2_done, mv2, ve2, rstd2, rstd2_done)):
                hold(pool, stats_done, u + 1)
                pool_a.mark(pool.tensor_scalar(ve[:, :], mv[:, :, 1], LN_EPS, None, ALU.add))
                pool_a.settle(pool, hold)
                pool.tensor_tensor(rstd[:, :], ve[:, :], minus_half[:, :], ALU.pow).then_inc(rstd_done, 1)
            out_rows = xn_dram[bass.ds(n * S + th * HALF, HALF), :].rearrange("(t p) n -> p t n", p=P)
            pool.dma_start(out_rows, xn[:, :, :]).then_inc(xn_out, DMA)
            pool_a.mark(pool.tensor_tensor(xin[:, :, :], xin[:, :, :], xn[:, :, :], ALU.add))
            pool_a.settle(pool, hold)
            for t in range(HT):
                last = pool.tensor_tensor(xin[:, t, :], xin[:, t, :], bo_sb[:, :], ALU.add)
            pool_a.mark(last)
            pool_a.settle(pool, hold)
            base_rows = out[bass.ds(n * S + th * HALF, HALF), :].rearrange("(t p) n -> p t n", p=P)
            pool.dma_start(base_rows, xin[:, :, :]).then_inc(base_out, DMA)
            pool_a.end()

        def set_v(b, hg):
            hold(pool, pv_done, (b * NG + hg - 1) * 2 * KT)
            pool.tensor_copy(v_ones[hg % 2][:, :, :, 0:HD],
                             v_sb[:, :, hg * HPG * HD:(hg + 1) * HPG * HD]
                             .rearrange("p t (j d) -> p t j d", j=HPG)).then_inc(v_ones_ready, 1)

        def squares(n, th):
            hold(pool, rotated, 2 * n + th + 1)
            for i in range(4):
                last = pool.tensor_tensor(rot[4 + i][:, :], qk[i][:, :], qk[i][:, :], ALU.mult)
            last.then_inc(sq_ready, 1)

        def divide(d):
            hold(pool, sums_in, (d + 1) * 8 * DMA)
            pool.tensor_tensor(num[:, :, :], num[:, :, :], rec[:, :, :], ALU.mult).then_inc(divided, 1)

        def attend(b, nxt, prev):
            set_v(b, 1)
            if nxt is not None:
                norm(nxt, 0)
            if prev is not None:
                divide(prev)
            set_v(b, 2)
            if nxt is not None:
                squares(nxt, 0)
                norm(nxt, 1)
            set_v(b, 3)
            if nxt is not None:
                squares(nxt, 1)
            if nxt is not None:
                hold(pool, side_free, nxt * JOBS + PJOB)
                set_v(nxt, 0)

        hold(pool, const_in, CONSTS * DMA)
        hold(pool, const_set, 3)
        norm(0, 0)
        squares(0, 0)
        norm(0, 1)
        squares(0, 1)
        hold(pool, side_free, PJOB)
        set_v(0, 0)
        attend(0, 1, None)
        with pool.Fori(1, NB - 1) as b:
            attend(b, b + 1, b - 1)
        attend(NB - 1, None, NB - 2)
        divide(NB - 1)
        hold(pool, base_out, 2 * DMA * NB)
        hold(pool, xn_out, 2 * DMA * NB)

    @block.scalar
    def _(act):
        def router(n, th):
            act.wait_ge(side_free, n * JOBS + HJOBS * th + 5)
            act.activation(lg_exp[:, :, :], lg[:, :, :], ACT.Exp).then_inc(lg_exped, 1)

        def attend(b, nxt, prev):
            for s in range(STEPS):
                at = b * STEPS + s
                for i in range(2):
                    act.wait_ge(qk_done[i], at + 1)
                    if i == 0:
                        need(act, pv_done, at - 1)
                    act.activation(probs[s % 2][:, 2 * i:2 * i + 2, :], score[i][:, :, :], ACT.Exp,
                                   scale=SCALE).then_inc(exp_done[i], 1)
                if nxt is not None and s in ROUTER_STEP:
                    router(nxt, ROUTER_STEP.index(s))

        router(0, 0)
        router(0, 1)
        act.wait_ge(weights_split, 1)
        attend(0, 1, None)
        with act.Fori(1, NB - 1) as b:
            attend(b, b + 1, b - 1)
        attend(NB - 1, None, NB - 2)

    @block.tensor
    def _(pe):
        def open_side(n, job):
            need(pe, side_free, n * JOBS + job - 1)
            return side[job % 2]

        def half_job(n, th, k):
            u, job = 2 * n + th, HJOBS * th + k
            cols = slice(th * HALF, (th + 1) * HALF)
            bank = open_side(n, job)
            if k < 4:
                src, ready, c = ((xn, xn_ready), (z, z_ready))[k // 2] + (k % 2,)
                pe.wait_ge(ready, u + 1)
                for t in range(HT):
                    last = pe.transpose(bank[:, t * P:(t + 1) * P], src[:, t, c * P:(c + 1) * P], ident_sb[:, :])
            elif k == 4:
                for t in range(HT):
                    for c in range(DC):
                        last = pe.matmul(bank[:, t * E:(t + 1) * E], xnT[:, c, t * P:(t + 1) * P],
                                         gate_sb[:, c, :], start=c == 0, stop=c == DC - 1)
            elif k == 9:
                pe.wait_ge(sq_ready, u + 1)
                for s in range(2):
                    for a in range(2):
                        last = pe.matmul(bank[s * KEYS_W:(s + 1) * KEYS_W, :], heads_sb[:, :],
                                         rot[4 + 2 * s + a][:, :], start=a == 0, stop=a == 1)
            else:
                w, a = ((WQ, 0), (WQ, 1), (WK, 0), (WK, 1))[k - 5]
                pe.wait_ge(zn_ready, u + 1)
                for i, (wt, zt) in enumerate(PASSES(w)):
                    for c in range(DC):
                        last = pe.matmul(bank[:, :], wt[:, c, a * P:(a + 1) * P], zt[:, c, cols],
                                         start=i == 0 and c == 0, stop=i == 2 and c == DC - 1)
            last.then_inc(side_full, 1)

        def PASSES(w):
            return (w_hi[w], zn_hi), (w_lo[w], zn_hi), (w_hi[w], zn_lo)

        def v_job(n, pair):
            bank = open_side(n, VJOB + pair)
            if pair == 0:
                pe.wait_ge(zn_ready, 2 * n + 2)
            for t2 in range(2):
                t = 2 * pair + t2
                for i, (wt, zt) in enumerate(PASSES(WV)):
                    for c in range(DC):
                        last = pe.matmul(bank[:, t2 * D:(t2 + 1) * D], zt[:, c, t * P:(t + 1) * P], wt[:, c, :],
                                         start=i == 0 and c == 0, stop=i == 2 and c == DC - 1)
            last.then_inc(side_full, 1)

        def peak_job(n, i):
            bank = open_side(n, PJOB + i)
            if i == 1:
                pe.wait_ge(v_peaked, n + 1)
            for c in range(2):
                last = pe.transpose(bank[0:1, c * P:(c + 1) * P], peaks[:, 2 * i + c:2 * i + c + 1], ident_sb[:, :])
            last.then_inc(side_full, 1)

        def wo_job(d, quarter):
            pe.wait_ge(at_split, QUARTERS * d + quarter + 1)
            if quarter > 0:
                pe.wait_ge(y_ready, QUARTERS * d + quarter)
            hi, lo = at_hi[quarter % 2], at_lo[quarter % 2]
            for t in range(2):
                for i, (at, wt) in enumerate(((hi, w_hi[WO]), (lo, w_hi[WO]), (hi, w_lo[WO]))):
                    for c in range(DC):
                        last = pe.matmul(wo_ps[:, t, :], at[:, c, t * P:(t + 1) * P], wt[:, c, :],
                                         start=i == 0 and c == 0, stop=i == 2 and c == DC - 1)
            last.then_inc(wo_done, 1)

        def maxima(b, hg, at):
            u, n = b * NG + hg, HPG * KT
            par = hg % 2
            for i in range(2):
                need(pe, exp_done[i], at)
            for k in range(n):
                j, t = k // KT, k % KT
                if k >= 2:
                    pe.wait_ge(max_free, u * n + k - 1)
                for kh in range(2):
                    last = pe.matmul(score[k % 2][:, kh, :], q_stack[par][0:ROWS, j, t * P:(t + 1) * P],
                                     k_stack[par][0:ROWS, j, kh * HALF:(kh + 1) * HALF], start=True, stop=True)
                last.then_inc(max_full, 1)
            pe.wait_ge(max_free, u * n + n)
            pe.transpose(score[0][0:n, 0, 0:P], row_max[:, :], ident_sb[:, :]).then_inc(max_turned, 1)
            pe.wait_ge(shift_in, (u + 1) * DMA)

        def pv(s, g_half=None, group=None):
            par, kt = (s // (2 * KT)) % 2, s % KT
            if kt == 0:
                need(pe, o_copied, g_half)
            if s % (2 * KT) == 0:
                pe.wait_ge(v_ones_ready, group + 1)
            for j in range(HPG):
                last = pe.matmul(o_ps[j * KEYS_W:(j + 1) * KEYS_W, :], v_ones[par][:, kt, j, :],
                                 probs[s % 2][:, j, :], start=kt == 0, stop=kt == KT - 1)
            last.then_inc(pv_done, 1)

        def turn_affinities():
            pe.wait_ge(aff_done, 2 * NB)
            pe.wait_ge(side_free, NB * JOBS)
            for t in range(TT):
                last = pe.transpose(side[t // HT][0:BE, (t % HT) * P:(t % HT + 1) * P], affinity[:, t, :],
                                    ident_sb[:, :])
            last.then_inc(aff_turned, 1)

        def attend(b, nxt, prev):
            wide = scores_wide(pe, b)
            for s in range(STEPS):
                at = b * STEPS + s
                hg, par, qh, kt = s // (2 * KT), (s // (2 * KT)) % 2, (s // KT) % 2, s % KT
                if s % (2 * KT) == 0:
                    pe.wait_ge(stack_in[par], (b * (NG // 2) + hg // 2 + 1) * 2 * len(Q_PARTS) * DMA)
                    with pe.If(wide):
                        maxima(b, hg, at)
                    with pe.Else():
                        passes_on(pe, (max_full, HPG * KT), (max_turned, 1))
                for i in range(2):
                    need(pe, exp_done[i], at)
                    for j in range(2):
                        last = pe.matmul(score[i][:, j, :], k_stack[par][0:FULL, 2 * i + j, kt * P:(kt + 1) * P],
                                         q_stack[par][0:FULL, 2 * i + j, qh * HALF:(qh + 1) * HALF],
                                         start=True, stop=True)
                    last.then_inc(qk_done[i], 1)
                if s > 0:
                    pv(s - 1, b * 2 * NG + (s - 1) // KT, b * NG + (s - 1) // (2 * KT))
                elif not isinstance(b, int) or b > 0:
                    pv(STEPS - 1)
                if prev is not None and s in WO_STEP:
                    wo_job(prev, WO_STEP.index(s))
                if nxt is not None:
                    for th in range(2):
                        for k in range(HJOBS):
                            if HALF_STEPS[th][k] == s:
                                half_job(nxt, th, k)
                    if s in V_STEP:
                        v_job(nxt, V_STEP.index(s))
                    if s in PEAK_STEP:
                        peak_job(nxt, PEAK_STEP.index(s))
                elif s == 0:
                    turn_affinities()

        pe.wait_ge(const_in, CONSTS * DMA)
        pe.wait_ge(weights_split, 1)
        pe.wait_ge(const_set, 3)
        pe.wait_ge(ones_set, 4)
        pe.wait_ge(zeros_set, 2)
        for th in range(2):
            for k in range(HJOBS):
                half_job(0, th, k)
        for pair in range(4):
            v_job(0, pair)
        for i in range(2):
            peak_job(0, i)
        attend(0, 1, None)
        with pe.Fori(1, NB - 1) as b:
            attend(b, b + 1, b - 1)
        attend(NB - 1, None, NB - 2)
        pe.wait_ge(exp_done[1], NB * STEPS)
        pv(STEPS - 1)
        for quarter in range(QUARTERS):
            wo_job(NB - 1, quarter)

    @block.vector
    def _(dve):
        def stats_of(n, src, mv, done):
            for t in range(HT):
                last = dve.bn_stats(stats[:, t, :], src[:, t, :])
            dve_a.mark(last)
            dve_a.settle(dve, hold)
            for t in range(HT):
                last = dve.bn_aggr(mv[:, t, :], stats[:, t, :])
            last.then_inc(done, 1)

        def scaled(to, src, mv, rstd, ready=None):
            for t in range(HT):
                last = dve.tensor_scalar(to[:, t, :], src[:, t, :], mv[:, t, 0:1], rstd[:, t:t + 1],
                                         ALU.subtract, ALU.mult)
            last.then_inc(ready, 1)

        def norm1(n, th):
            u = 2 * n + th
            dve_a.start(u)
            dve.wait_ge(x_in, DMA * (u + 1))
            stats_of(n, xin, mv1, stats1_done)

        def norm2(n, th):
            u = 2 * n + th
            dve.wait_ge(rstd1_done, u + 1)
            need(dve, xn_out, DMA * u)
            scaled(xn, xin, mv1, rstd1, xn_ready)
            dve.wait_ge(xn_ready, u + 1)
            stats_of(n, xn, mv2, stats2_done)

        def norm3(n, th):
            dve.wait_ge(rstd2_done, 2 * n + th + 1)
            scaled(z, xn, mv2, rstd2, z_ready)

        def take(n, job):
            dve.wait_ge(side_full, n * JOBS + job + 1)
            return side[job % 2]

        def turned_x(n, th, c):
            job = HJOBS * th + c
            bank = take(n, job)
            if th == 0 and c == 0:
                need(dve, rec_out, (n - 1) * DMA)
            dve.tensor_copy(xnT[:, c, :], bank[:, :]).then_inc(side_free, 1)

        def turned_z(n, th, c):
            bank = take(n, HJOBS * th + 2 + c)
            dve.tensor_scalar(znT[:, c, :], bank[:, :], lnw_sb[:, c:c + 1], lnb_sb[:, c:c + 1],
                              ALU.mult, ALU.add).then_inc(side_free, 1)
            if c == DC - 1:
                cols = slice(th * HALF, (th + 1) * HALF)
                dve.wait_ge(side_free, n * JOBS + HJOBS * th + 4)
                dve_a.mark(dve.tensor_copy(zn_hi[:, :, cols], znT[:, :, :]))
                dve_a.settle(dve)
                dve.tensor_tensor(zn_lo[:, :, cols], znT[:, :, :], zn_hi[:, :, cols], ALU.subtract)\
                   .then_inc(zn_ready, 1)

        def logits(n, th):
            bank = take(n, HJOBS * th + 4)
            view = bank[:, 0:HT * E].rearrange("p (t e) -> p t e", e=E)
            dve_a.mark(dve.tensor_reduce(lg_max[:, :], view, AX_X, ALU.max))
            dve_a.settle(dve)
            dve.tensor_tensor(lg[:, :, :], view, lg_max[:, :].unsqueeze(2).to_broadcast([P, HT, E]),
                              ALU.subtract).then_inc(side_free, 1)

        def affinities(n, th):
            u = 2 * n + th
            dve.wait_ge(lg_exped, u + 1)
            dve_a.mark(dve.tensor_reduce(lg_sum[:, :], lg_exp[:, :, :], AX_X, ALU.add))
            dve_a.settle(dve)
            dve_a.mark(dve.reciprocal(lg_rec[:, :], lg_sum[:, :]))
            dve_a.settle(dve)
            for t in range(HT):
                last = dve.tensor_scalar(affinity[:, th * HT + t, bass.ds(n * E, E)], lg_exp[:, t, :],
                                         lg_rec[:, t:t + 1], None, ALU.mult)
            last.then_inc(aff_done, 1)

        def biased(n, th, k):
            bank = take(n, HJOBS * th + 5 + k)
            bias = (bq_sb, bk_sb)[k // 2]
            dve.tensor_scalar(qk[k][:, :], bank[:, :], bias[:, k % 2:k % 2 + 1], None, ALU.add)\
               .then_inc(side_free, 1)

        def rotary(n, th, s):
            cols = slice(th * HALF, (th + 1) * HALF)
            dve.wait_ge(side_free, n * JOBS + HJOBS * th + 7 + 2 * s)
            a, b, t = qk[2 * s], qk[2 * s + 1], rot[4 * s:4 * s + 4]
            for i, (v, tab) in enumerate(((a, cos_sb), (b, sin_sb), (a, sin_sb), (b, cos_sb))):
                last = dve.tensor_tensor(t[i][:, :], v[:, :], tab[:, cols], ALU.mult)
            dve_a.mark(last)
            dve_a.settle(dve)
            dve.tensor_tensor(a[:, :], t[0][:, :], t[1][:, :], ALU.subtract)
            last = dve.tensor_tensor(b[:, :], t[2][:, :], t[3][:, :], ALU.add)
            if s == 0:
                dve_a.mark(last)
            else:
                last.then_inc(rotated, 1)

        def norm_peaks(n, th):
            bank = take(n, HJOBS * th + 9)
            dve.tensor_reduce(peaks[0:2 * KEYS_W, th:th + 1], bank[0:2 * KEYS_W, :], AX_X, ALU.max)\
               .then_inc(side_free, 1)

        def value_peaks(n):
            dve.wait_ge(side_free, n * JOBS + PJOB)
            for i, op in enumerate((ALU.max, ALU.min)):
                last = dve.tensor_reduce(peaks[:, 2 + i:3 + i], v_sb[:, :, :].rearrange("p t d -> p (t d)"), AX_X, op)
            last.then_inc(v_peaked, 1)

        def limits(n):
            dve_f.start(n)
            bank = take(n, PJOB)
            dve.tensor_reduce(norms[:, :], bank[0:1, 0:2 * P].rearrange("o (h c) -> o c h", h=2), AX_X, ALU.max)\
               .then_inc(side_free, 1)
            bank = take(n, PJOB + 1)
            dve.tensor_scalar(terms[:, KEYS_W:KEYS_W + P], bank[0:1, 0:P], LIMIT / VALUE_LIMIT, None, ALU.mult)
            dve.tensor_scalar(terms[:, KEYS_W + P:KEYS_W + 2 * P], bank[0:1, P:2 * P], -LIMIT / VALUE_LIMIT, None,
                              ALU.mult).then_inc(side_free, 1)
            dve.wait_ge(side_free, (n + 1) * JOBS)
            dve_f.mark(dve.tensor_tensor(terms[:, 0:KEYS_W], norms[:, 0:KEYS_W], norms[:, KEYS_W:2 * KEYS_W], ALU.mult))
            dve_f.settle(dve)
            to = bound[:, n:n + 1] if isinstance(n, int) else bound[:, bass.ds(n, 1)]
            dve_f.mark(dve.tensor_reduce(to, terms[:, :], AX_X, ALU.max))
            dve_f.settle(dve, hold)
            dve_f.mark(dve.tensor_copy(terms[:, KEYS_W + 2 * P:], to))
            dve_f.settle(dve)
            dve.sem_inc(bound_ready, 1)
            dve_f.end()

        def split(n, th, s):
            u = 2 * n + th
            if s == 0:
                need(dve, parts_out, u * PARTS_DMA)
                dve.wait_ge(rotated, u + 1)
            to, rest = parts[s], rot[2 * s:2 * s + 2]
            for i in range(2):
                last = dve.tensor_copy(to[:, 0, i, :], qk[2 * s + i][:, :])
            dve_a.mark(last)
            dve_a.settle(dve)
            for i in range(2):
                last = dve.tensor_tensor(rest[i][:, :], qk[2 * s + i][:, :], to[:, 0, i, :], ALU.subtract)
            dve_a.mark(last)
            dve_a.settle(dve)
            for i in range(2):
                last = dve.tensor_copy(to[:, 1, i, :], rest[i][:, :])
            dve_a.mark(last)
            dve_a.settle(dve)
            for i in range(2):
                last = dve.tensor_tensor(to[:, 2, i, :], rest[i][:, :], to[:, 1, i, :], ALU.subtract)
            if s == 0:
                dve_a.mark(last)
            else:
                last.then_inc(parts_ready, 1)
                dve_a.end()

        def values(n, pair):
            bank = take(n, VJOB + pair)
            if pair == 0:
                need(dve, v_ones_ready, NG * n)
            for t in range(2):
                last = dve.tensor_tensor(v_sb[:, 2 * pair + t, :], bank[:, t * D:(t + 1) * D], bv_sb[:, :], ALU.add)
            last.then_inc(side_free, 1)

        def half_job(n, th, k):
            if k < 2:
                turned_x(n, th, k)
            elif k < 4:
                turned_z(n, th, k - 2)
            elif k == 4:
                logits(n, th)
            elif k == 9:
                norm_peaks(n, th)
            else:
                biased(n, th, k - 5)

        def copy_o(b, il):
            i = b * 2 * NG + il
            dve.wait_ge(pv_done, (i + 1) * KT)
            need(dve, o_out[il % 2], (b * NG + il // 2) * DMA)
            dve.tensor_copy(o_sb[il % 2][:, :], o_ps[:, :]).then_inc(o_copied, 1)


        def invert(d):
            dve.wait_ge(den_in, (d + 1) * DMA)
            dve.reciprocal(den_rec, den).then_inc(den_done, 1)

        def quarter_split(d, quarter):
            cols = slice(quarter * 2 * P, (quarter + 1) * 2 * P)
            if quarter == 0:
                dve_d.start(d)
                dve.wait_ge(divided, d + 1)
                dve.wait_ge(base_in, (d + 1) * DMA)
            dve_d.mark(dve.tensor_copy(at_hi[quarter % 2][:, :, :], num[:, :, cols]))
            dve_d.settle(dve)
            dve.tensor_tensor(at_lo[quarter % 2][:, :, :], num[:, :, cols], at_hi[quarter % 2][:, :, :],
                              ALU.subtract).then_inc(at_split, 1)
            if quarter == QUARTERS - 1:
                dve_d.end()

        def add_base(d, quarter):
            dve.wait_ge(wo_done, QUARTERS * d + quarter + 1)
            rows = base[:, 2 * quarter:2 * quarter + 2, :]
            dve.tensor_tensor(rows, wo_ps[:, :, :], rows, ALU.add).then_inc(y_ready, 1)

        def maxima(b, hg):
            u, n = b * NG + hg, HPG * KT
            dve_b.start(u)
            for k in range(n):
                dve.wait_ge(max_full, u * n + k + 1)
                dve.tensor_reduce(row_max[:, k:k + 1], score[k % 2][:, :, :].rearrange("p a n -> p (a n)"),
                                  AX_X, ALU.max).then_inc(max_free, 1)
            dve.wait_ge(max_turned, u + 1)
            need(dve, shift_out, DMA * u)
            dve_b.mark(dve.tensor_scalar(neg_max[:, :], score[0][0:n, 0, 0:P], -1.0, None, ALU.mult))
            dve_b.settle(dve)
            dve_b.mark(dve.tensor_copy(shift[:, 0, :], neg_max[:, :]))
            dve_b.settle(dve)
            dve_b.mark(dve.tensor_tensor(neg_rest[:, :], neg_max[:, :], shift[:, 0, :], ALU.subtract))
            dve_b.settle(dve)
            dve_b.mark(dve.tensor_copy(shift[:, 1, :], neg_rest[:, :]))
            dve_b.settle(dve)
            dve.tensor_tensor(shift[:, 2, :], neg_rest[:, :], shift[:, 1, :], ALU.subtract).then_inc(shift_ready, 1)
            dve_b.end()

        def affinities_in():
            dve.wait_ge(aff_turned, 1)
            for half in range(2):
                last = dve.tensor_copy(top_scores[:, half * HALF:(half + 1) * HALF], side[half][0:BE, :])
            last.then_inc(top_copied, 1)
            dve.wait_ge(top_copied, 1)
            dve_t.start(0)

        def take_top(op):
            eight = slice(8 * (op // 3), 8 * (op // 3) + 8)
            if op > 0:
                dve_t.settle(dve)
            if op % 3 == 0:
                dve_t.mark(dve.max(top_gate[:, eight], top_scores))
            elif op % 3 == 1:
                dve_t.mark(dve.max_index(top_row[:, eight], top_gate[:, eight], top_scores))
            else:
                dve_t.mark(dve.match_replace(top_scores, top_gate[:, eight], top_scores, -1.0))

        def attend(b, nxt, prev):
            wide = scores_wide(dve, b)
            for s in range(STEPS):
                if s % (2 * KT) == 0:
                    with dve.If(wide):
                        maxima(b, s // (2 * KT))
                    with dve.Else():
                        passes_on(dve, (max_free, HPG * KT), (dve_b.sem, dve_b.per), (shift_ready, 1))
                if s % KT == 0:
                    if s > 0:
                        copy_o(b, s // KT - 1)
                    elif prev is not None:
                        copy_o(prev, 2 * NG - 1)
                if prev is not None:
                    if s == DEN_STEP:
                        invert(prev)
                    if s == SUMS_STEP:
                        quarter_split(prev, 0)
                        quarter_split(prev, 1)
                    if s in WO_STEP:
                        quarter = WO_STEP.index(s)
                        add_base(prev, quarter)
                        if quarter + 2 < QUARTERS:
                            quarter_split(prev, quarter + 2)
                if nxt is not None:
                    for th, at in enumerate(NORM_STEP):
                        if s == at:
                            norm1(nxt, th)
                        if s == at + 2:
                            norm2(nxt, th)
                        if s == at + 4:
                            norm3(nxt, th)
                        for k in range(HJOBS):
                            if HALF_STEPS[th][k] == s:
                                half_job(nxt, th, k)
                        if s == PARTS_STEP[th]:
                            affinities(nxt, th)
                        for i in range(2):
                            if s == PARTS_STEP[th] + i:
                                rotary(nxt, th, i)
                            if s == PARTS_STEP[th] + 4 + i:
                                split(nxt, th, i)
                    if s in V_STEP:
                        values(nxt, V_STEP.index(s))
                    if s == V_STEP[-1]:
                        value_peaks(nxt)
                    if s == PEAK_STEP[-1]:
                        limits(nxt)
                else:
                    if s == 0:
                        affinities_in()
                    for op in range(TOP_OPS * s // STEPS, TOP_OPS * (s + 1) // STEPS):
                        take_top(op)

        for i in range(2):
            dve.memset(k_stack[i][SHIFT:FULL, :, :], 1.0).then_inc(ones_set, 1)
            dve.memset(q_stack[i][SHIFT:FULL, :, :], 0.0).then_inc(ones_set, 1)
        dve.memset(peaks[:, :], 0.0).then_inc(zeros_set, 1)
        dve.memset(terms[:, :], 0.0).then_inc(zeros_set, 1)
        dve.wait_ge(zeros_set, 2)
        dve.wait_ge(weights_in, 4 * DMA)
        raw = [probs[0][:, i, :].rearrange("p (c n) -> p c n", c=DC) for i in range(4)]
        for i in range(4):
            last = dve.tensor_copy(w_hi[i][:, :, :], raw[i])
        last.then_inc(weights_high, 1)
        dve.wait_ge(weights_high, 1)
        for i in range(4):
            last = dve.tensor_tensor(w_lo[i][:, :, :], raw[i], w_hi[i][:, :, :], ALU.subtract)
        last.then_inc(weights_split, 1)
        dve.wait_ge(const_in, CONSTS * DMA)
        for th in range(2):
            norm1(0, th)
            norm2(0, th)
            norm3(0, th)
            for k in range(9):
                half_job(0, th, k)
            affinities(0, th)
            for s in range(2):
                rotary(0, th, s)
            for s in range(2):
                split(0, th, s)
            half_job(0, th, 9)
        for pair in range(4):
            values(0, pair)
        value_peaks(0)
        limits(0)
        attend(0, 1, None)
        with dve.Fori(1, NB - 1) as b:
            attend(b, b + 1, b - 1)
        attend(NB - 1, None, NB - 2)
        copy_o(NB - 1, 2 * NG - 1)
        invert(NB - 1)
        quarter_split(NB - 1, 0)
        quarter_split(NB - 1, 1)
        for quarter in range(QUARTERS):
            add_base(NB - 1, quarter)
            if quarter + 2 < QUARTERS:
                quarter_split(NB - 1, quarter + 2)


def expert_part(nc, ctx, g):
    (T, D, NB, S, DC, E, CAP, BE, F, FC) = (g[k] for k in "T D NB S DC E CAP BE F FC".split())
    out, xn_dram, wg, wu, wd = (g[k] for k in "out xn_dram wg wu wd".split())
    ident_sb, row0_sb, top_gate, top_row = (g[k] for k in "ident_sb row0_sb top_gate top_row".split())
    SLOTS = 4 * P
    ST = SLOTS // P
    HALVES = CAP // P
    UNITS = NB * HALVES // ST
    COLS = NB * HALVES

    def sb(name, shape, dt=F32):
        return ctx.enter_context(nc.sbuf_tensor(name, shape, dt))

    def ps(name, shape):
        return ctx.enter_context(nc.psum_tensor(name, shape, F32))

    def sem(name):
        return ctx.enter_context(nc.semaphore(name))

    row_f = sb("row_f", [BE, CAP])
    rows_all = sb("rows_all", [P, E, NB, HALVES], U32)
    gates_all = sb("gates_all", [P, E, NB, HALVES])
    rows_flat = rows_all[:, :, :, :].rearrange("p e b h -> p (e b h)")
    gates_flat = gates_all[:, :, :, :].rearrange("p e b h -> p (e b h)")
    rows_now = [sb(f"rows_now{i}", [P, ST], U32) for i in range(UNITS)]
    shapes = ([P, DC, F], [P, DC, F], [P, FC, D])
    w_raw = [sb(f"w_raw{i}", s) for i, s in enumerate(shapes)]
    w_hi = [[sb(f"we_hi{k}{i}", s, F32R) for i, s in enumerate(shapes)] for k in range(2)]
    w_lo = [[sb(f"we_lo{k}{i}", s, F32R) for i, s in enumerate(shapes)] for k in range(2)]
    GATE, UP, DOWN = range(3)
    WEIGHTS = len(shapes)
    xs = [sb(f"xs{i}", [P, ST, D]) for i in range(2)]
    x_hi, x_lo = sb("x_hi", [P, DC, SLOTS], F32R), sb("x_lo", [P, DC, SLOTS], F32R)
    silu = [sb(f"silu{i}", [P, SLOTS]) for i in range(2)]
    h = [sb(f"h{i}", [P, SLOTS]) for i in range(2)]
    h_hi, h_lo = sb("h_hi", [P, FC, SLOTS], F32R), sb("h_lo", [P, FC, SLOTS], F32R)
    y = [[sb(f"y{i}{t}", [P, D]) for t in range(ST)] for i in range(2)]

    g_ps = [ps(f"g_ps{i}", [P, SLOTS]) for i in range(2)]
    u_ps = [ps(f"u_ps{i}", [P, SLOTS]) for i in range(2)]
    xt_ps = [ps(f"xt_ps{i}", [P, SLOTS]) for i in range(DC)]
    d_ps = [ps(f"d_ps{i}", [P, SLOTS]) for i in range(2)]

    row_cast, row_added, top_turned, top_spread = (
        sem(n) for n in ("row_cast", "row_added", "top_turned", "top_spread"))
    w_in, w_high, w_split = sem("w_in"), sem("w_high"), sem("w_split")
    rows_set = sem("rows_set")
    gathered = [sem(f"gathered{i}") for i in range(2)]
    scattered = [sem(f"scattered{i}") for i in range(UNITS)]
    xt_full, x_high, x_split = sem("xt_full"), sem("x_high"), sem("x_split")
    gu_full, silu_done, h_done, h_high, h_split = (
        sem(n) for n in ("gu_full", "silu_done", "h_done", "h_high", "h_split"))
    down_full, y_scaled = sem("down_full"), sem("y_scaled")
    passed = sem("passed_e")

    def need(eng, s, value):
        if not isinstance(value, int) or value > 0:
            eng.wait_ge(s, value)

    def hold(eng, s, value):
        need(eng, s, value)
        if not isinstance(value, int):
            eng.sem_inc(passed, 1)

    def experts(eng, pair):
        pair(0, False)
        with eng.Fori(1, E // 2 - 1) as p:
            pair(p, False)
        pair(E // 2 - 1, True)

    block = ctx.enter_context(nc.Block())

    @block.sync
    def _(sp):
        def load(e):
            for raw, dram in zip(w_raw, (wg, wu, wd)):
                sp.dma_start(raw[:, :, :], dram[e].rearrange("(c p) n -> p c n", p=P)).then_inc(w_in, DMA)

        def pair(p, last):
            for k in range(2):
                if not (last and k == 1):
                    hold(sp, w_split, WEIGHTS * (2 * p + k + 1))
                    load(2 * p + k + 1)

        load(0)
        experts(sp, pair)

    @block.gpsimd
    def _(pool):
        def gather(e, bp, par):
            unit = UNITS * e + bp
            need(pool, scattered[bp], ST * DMA * e)
            hold(pool, xt_full, DC * (unit - 1))
            pool.tensor_copy(rows_now[bp][:, :], rows_flat[:, bass.ds(e * COLS + bp * ST, ST)]).then_inc(rows_set, 1)
            hold(pool, rows_set, unit + 1)
            for t in range(ST):
                pool.indirect_dma_start(xs[par][:, t, :], None, xn_dram[:, :],
                                        bass.IndirectOffsetOnAxis(ap=rows_now[bp][:, t:t + 1], axis=0))\
                    .then_inc(gathered[par], DMA)

        def scatter(e, bp, par):
            unit = UNITS * e + bp
            for t in range(ST):
                hold(pool, y_scaled, ST * unit + t + 1)
                pool.indirect_dma_start(out[:, :], bass.IndirectOffsetOnAxis(ap=rows_now[bp][:, t:t + 1], axis=0),
                                        y[par][t][:, :], None, compute_op=ALU.add)\
                    .then_inc(scattered[bp], DMA)

        def pair(p, last):
            for k in range(2):
                for bp in range(UNITS):
                    e, n = 2 * p + k, k * UNITS + bp
                    if not (last and n == 2 * UNITS - 1):
                        gather(e + (bp + 1) // UNITS, (bp + 1) % UNITS, (n + 1) % 2)
                    scatter(e, bp, n % 2)

        pool.wait_ge(top_spread, 2 * HALVES)
        gather(0, 0, 0)
        experts(pool, pair)
        for bp in range(UNITS):
            pool.wait_ge(scattered[bp], ST * DMA * E)

    @block.scalar
    def _(act):
        def split_w(e, k, m):
            act.wait_ge(w_in, 3 * DMA * (e + 1))
            act.copy(w_hi[k][m][:, :, :], w_raw[m][:, :, :]).then_inc(w_high, 1)

        def turned(unit):
            for c in range(DC):
                act.wait_ge(xt_full, DC * unit + c + 1)
                act.copy(x_hi[:, c, :], xt_ps[c][:, :]).then_inc(x_high, 1)

        def high(unit, f):
            act.wait_ge(h_done, FC * unit + f + 1)
            act.copy(h_hi[:, f, :], h[f % 2][:, :]).then_inc(h_high, 1)

        def pair(p, last):
            for k in range(2):
                for bp in range(UNITS):
                    unit = UNITS * (2 * p + k) + bp
                    for f in range(FC):
                        act.wait_ge(gu_full, FC * unit + f + 1)
                        act.activation(silu[f % 2][:, :], g_ps[f % 2][:, :], ACT.Silu).then_inc(silu_done, 1)
                        if f > 0:
                            high(unit, f - 1)
                    high(unit, FC - 1)
                    if not (last and k == 1 and bp == UNITS - 1):
                        turned(unit + 1)
                    if bp < WEIGHTS and not (last and k == 1):
                        split_w(2 * p + k + 1, 1 - k, bp)

        turned(0)
        for m in range(WEIGHTS):
            split_w(0, 0, m)
        experts(act, pair)

    @block.tensor
    def _(pe):
        def turn(unit, par):
            pe.wait_ge(gathered[par], ST * DMA * ((unit - par) // 2 + 1) if isinstance(unit, int)
                       else (unit - par) * (ST * DMA // 2) + ST * DMA)
            for c in range(DC):
                need(pe, x_split, DC * unit + c - 1)
                for t in range(ST):
                    last = pe.transpose(xt_ps[c][:, t * P:(t + 1) * P], xs[par][:, t, c * P:(c + 1) * P], ident_sb[:, :])
                last.then_inc(xt_full, 1)

        def gate_up(unit, k):
            pe.wait_ge(x_split, DC * unit + DC)
            for f in range(FC):
                need(pe, h_done, FC * unit + f - 1)
                for w, bank in ((GATE, g_ps), (UP, u_ps)):
                    for i, (wt, xt) in enumerate(((w_hi, x_hi), (w_lo, x_hi), (w_hi, x_lo))):
                        for c in range(DC):
                            last = pe.matmul(bank[f % 2][:, :], wt[k][w][:, c, f * P:(f + 1) * P], xt[:, c, :],
                                             start=i == 0 and c == 0, stop=i == 2 and c == DC - 1)
                last.then_inc(gu_full, 1)

        def down(unit, k):
            def part(t, fs):
                for f in fs:
                    pe.wait_ge(h_split, FC * unit + f + 1)
                    for i, (ht, wt) in enumerate(((h_hi, w_hi), (h_lo, w_hi), (h_hi, w_lo))):
                        last = pe.matmul(d_ps[t % 2][:, 0:D], ht[:, f, t * P:(t + 1) * P], wt[k][DOWN][:, f, :],
                                         start=i == 0 and f == 0, stop=i == 2 and f == FC - 1)
                return last

            for t in range(2):
                need(pe, y_scaled, ST * unit + t - 1)
                part(t, range(FC - 1))
            for t in range(2):
                part(t, (FC - 1,)).then_inc(down_full, 1)
            for t in range(2, ST):
                pe.wait_ge(y_scaled, ST * unit + t - 1)
                part(t, range(FC)).then_inc(down_full, 1)

        def pair(p, last):
            for k in range(2):
                for bp in range(UNITS):
                    e, n = 2 * p + k, k * UNITS + bp
                    unit = UNITS * e + bp
                    if bp == 0:
                        pe.wait_ge(w_split, WEIGHTS * (e + 1))
                    gate_up(unit, k)
                    if not (last and n == 2 * UNITS - 1):
                        turn(unit + 1, (n + 1) % 2)
                    down(unit, k)

        pe.wait_ge(row_added, 1)
        for i, src in enumerate((row_f, top_gate)):
            for half in range(HALVES):
                last = pe.transpose(d_ps[i][:, half * BE:(half + 1) * BE], src[:, half * P:(half + 1) * P],
                                    ident_sb[0:BE, 0:BE])
        last.then_inc(top_turned, 1)
        turn(0, 0)
        experts(pe, pair)

    @block.vector
    def _(dve):
        def split_w(e, k, m):
            dve.wait_ge(w_high, WEIGHTS * e + m + 1)
            dve.tensor_tensor(w_lo[k][m][:, :, :], w_raw[m][:, :, :], w_hi[k][m][:, :, :], ALU.subtract)\
               .then_inc(w_split, 1)

        def turned(unit):
            for c in range(DC):
                dve.wait_ge(x_high, DC * unit + c + 1)
                dve.tensor_tensor(x_lo[:, c, :], xt_ps[c][:, :], x_hi[:, c, :], ALU.subtract).then_inc(x_split, 1)

        def low(unit, f):
            dve.wait_ge(h_high, FC * unit + f + 1)
            dve.tensor_tensor(h_lo[:, f, :], h[f % 2][:, :], h_hi[:, f, :], ALU.subtract).then_inc(h_split, 1)

        def pair(p, last):
            for k in range(2):
                for bp in range(UNITS):
                    e, n = 2 * p + k, k * UNITS + bp
                    unit = UNITS * e + bp
                    for f in range(FC):
                        dve.wait_ge(silu_done, FC * unit + f + 1)
                        need(dve, h_split, FC * unit + f - 1)
                        dve.tensor_tensor(h[f % 2][:, :], u_ps[f % 2][:, :], silu[f % 2][:, :], ALU.mult)\
                           .then_inc(h_done, 1)
                        if f > 0:
                            low(unit, f - 1)
                    low(unit, FC - 1)
                    if not (last and n == 2 * UNITS - 1):
                        turned(unit + 1)
                    if bp < WEIGHTS and not (last and k == 1):
                        split_w(e + 1, 1 - k, bp)
                    need(dve, scattered[(bp - 2) % UNITS], ST * DMA * (e + (bp >= 2)))
                    for t in range(ST):
                        dve.wait_ge(down_full, ST * unit + t + 1)
                        dve.tensor_scalar(y[n % 2][t][:, :], d_ps[t % 2][:, 0:D],
                                          gates_flat[:, bass.ds(e * COLS + bp * ST + t, 1)], None, ALU.mult)\
                           .then_inc(y_scaled, 1)

        dve.tensor_copy(row_f[:, :], top_row[:, :]).then_inc(row_cast, 1)
        dve.wait_ge(row_cast, 1)
        dve.tensor_scalar(row_f[:, :], row_f[:, :], row0_sb[:, :], None, ALU.add).then_inc(row_added, 1)
        dve.wait_ge(top_turned, 1)
        for i, to in enumerate((rows_all, gates_all)):
            for half in range(HALVES):
                dve.tensor_copy(to[:, :, :, half], d_ps[i][:, half * BE:(half + 1) * BE]
                                .rearrange("p (b e) -> p e b", e=E)).then_inc(top_spread, 1)
        dve.wait_ge(top_spread, 2 * HALVES)
        turned(0)
        for m in range(WEIGHTS):
            split_w(0, 0, m)
        experts(dve, pair)


def kernel(**inputs):
    import numpy as np
    import concourse.bacc as bacc
    from concourse.bass_utils import run_bass_kernel_spmd as run

    x = np.ascontiguousarray(inputs["L0_attn_x"])
    NB, S, D = x.shape
    HD = D // NHEAD
    order = np.arange(D).reshape(NHEAD, HD // 2, 2).transpose(2, 0, 1).reshape(D)
    inv_freq = np.float32(1.0) / np.float32(10000.0) ** (np.arange(0, HD, 2, dtype=np.float32) / np.float32(HD))
    angle = np.outer(np.arange(S, dtype=np.float32), inv_freq).astype(np.float32)

    def columns(v):
        return v.reshape(-1, P).T

    arrays = {
        "x": x.reshape(NB * S, D),
        "ln_w": columns(inputs["L0_attn_ln_w"]), "ln_b": columns(inputs["L0_attn_ln_b"]),
        "wq_t": inputs["L0_attn_Wq"].T[:, order], "wk_t": inputs["L0_attn_Wk"].T[:, order],
        "wv_t": inputs["L0_attn_Wv"].T, "wo_t": inputs["L0_attn_Wo"].T,
        "bq": columns(inputs["L0_attn_bq"][order]), "bk": columns(inputs["L0_attn_bk"][order]),
        "bv": inputs["L0_attn_bv"], "bo": inputs["L0_attn_bo"],
        "gate_w": inputs["L0_ffn_gate_w"],
        "wg": inputs["L0_ffn_Wg"], "wu": inputs["L0_ffn_Wu"], "wd": inputs["L0_ffn_Wd"],
        "cos": np.tile(np.cos(angle).T, (NHEAD, 1)), "sin": np.tile(np.sin(angle).T, (NHEAD, 1)),
        "ident": np.eye(P, dtype=np.float32),
        "heads": (np.arange(P)[:, None] // (HD // 2) == np.arange(KEYS_W)[None, :]).astype(np.float32),
        "row0": np.repeat(np.arange(NB, dtype=np.float32) * S, NEXPERT)[:, None],
    }
    arrays = {k: np.ascontiguousarray(v) for k, v in arrays.items()}
    nc = bacc.Bacc("TRN2", target_bir_lowering=False, num_devices=1)
    args = {k: nc.dram_tensor(f"in_{k}", v.shape, mybir.dt.from_np(v.dtype), kind="ExternalInput").ap()
            for k, v in arrays.items()}
    out = nc.dram_tensor("out_0", (NB * S, D), F32, kind="ExternalOutput").ap()
    build(nc, **args, out=out)
    r = run(nc, [{f"in_{k}": v for k, v in arrays.items()}], core_ids=[0])
    return r.results[0]["out_0"].reshape(NB, S, D)
```

```python
from contextlib import ExitStack

import concourse.bass as bass
import numpy as np
from concourse import mybir

ACT = mybir.ActivationFunctionType
ALU = mybir.AluOpType
AX_X = mybir.AxisListType.X
F32 = mybir.dt.float32
F32R = mybir.dt.float32r
BF16 = mybir.dt.bfloat16
U32 = mybir.dt.uint32

P = 128
LN_EPS = 1e-5
NHEAD = 16
NEXPERT = 8
DMA = 16
HPG = 4
KEYS_W = 32
NPART = 3

RUNS = (3, 2, 1)

SCORE_LIMIT = 78.0
VALUE_LIMIT = 20.0


class Tally:

    def __init__(self, sem, per):
        self.sem, self.per, self.base, self.count = sem, per, 0, 0

    def start(self, n):
        self.base, self.count = n * self.per, 0

    def mark(self, instruction):
        instruction.then_inc(self.sem, 1)
        self.count += 1
        assert self.count <= self.per

    def settle(self, eng, wait=None):
        if wait:
            wait(eng, self.sem, self.base + self.count)
        else:
            eng.wait_ge(self.sem, self.base + self.count)

    def end(self):
        assert self.count == self.per, (self.count, self.per)


def build(nc, x, ln_w, ln_b, wq_t, wk_t, wv_t, wo_t, bq, bk, bv, bo, gate_w, wg, wu, wd,
          cos, sin, ident, row0, heads, out):
    T, D = x.shape
    NB = 8
    S = T // NB
    TT = S // P
    DC = D // P
    HALF = S // 2
    HT = HALF // P
    HD = D // NHEAD
    HR = HD // 2
    NG = NHEAD // HPG
    KT = S // P
    STEPS = NG * 2 * KT
    ROWS = sum(RUNS) * HD
    SHIFT = ROWS
    FULL = ROWS + NPART
    SCALE = float(HD) ** -0.5
    E = NEXPERT
    CAP = 2 * S // E
    BE = NB * E
    F = wg.shape[2]
    FC = F // P

    q_dram = nc.dram_tensor("q_parts", (NB, NPART, 2, HR, NHEAD, S), BF16).ap()
    k_dram = nc.dram_tensor("k_parts", (NB, NPART, 2, HR, NHEAD, S), BF16).ap()
    shift_dram = nc.dram_tensor("shift_parts", (NB, NG, NPART, HPG * KT, P), BF16).ap()
    o_dram = nc.dram_tensor("o_sums", (NB, 2, NG, HPG, 2, HD, HALF), F32).ap()
    rec_dram = nc.dram_tensor("den_recs", (NB, 2, NHEAD, HALF), F32).ap()
    xn_dram = nc.dram_tensor("xn_rows", (T, D), F32).ap()

    outer = ExitStack()
    with outer:
        def sem(name):
            return outer.enter_context(nc.semaphore(name))

        def keep(name, shape, dt):
            return outer.enter_context(nc.sbuf_tensor(name, shape, dt))

        ident_sb = keep("ident_sb", [P, P], F32)
        row0_sb = keep("row0_sb", [BE, 1], F32)
        affinity = keep("affinity", [P, TT, BE], F32)
        top_gate = keep("top_gate", [BE, CAP], F32)
        top_row = keep("top_row", [BE, CAP], U32)

        with ExitStack() as inner:
            attention_part(nc, inner, locals())
        with ExitStack() as inner:
            expert_part(nc, inner, locals())


def attention_part(nc, ctx, g):
    (T, D, NB, S, TT, DC, HALF, HT, HD, HR, NG, KT, STEPS, ROWS, SHIFT, FULL, SCALE, E, CAP, BE) = (
        g[k] for k in "T D NB S TT DC HALF HT HD HR NG KT STEPS ROWS SHIFT FULL SCALE E CAP BE".split())
    x, out, q_dram, k_dram, shift_dram, o_dram, rec_dram, xn_dram = (
        g[k] for k in "x out q_dram k_dram shift_dram o_dram rec_dram xn_dram".split())
    ident_sb, row0_sb, affinity, top_gate, top_row = (
        g[k] for k in "ident_sb row0_sb affinity top_gate top_row".split())

    def sb(name, shape, dt=F32):
        return ctx.enter_context(nc.sbuf_tensor(name, shape, dt))

    def ps(name, shape):
        return ctx.enter_context(nc.psum_tensor(name, shape, F32))

    def sem(name):
        return ctx.enter_context(nc.semaphore(name))

    w_hi = [sb(f"w_hi{i}", [P, DC, D], F32R) for i in range(4)]
    w_lo = [sb(f"w_lo{i}", [P, DC, D], F32R) for i in range(4)]
    WQ, WK, WV, WO = range(4)
    cos_sb, sin_sb = sb("cos_sb", [P, S]), sb("sin_sb", [P, S])
    gate_sb = sb("gate_sb", [P, DC, E])
    lnw_sb, lnb_sb = sb("lnw_sb", [P, DC]), sb("lnb_sb", [P, DC])
    bq_sb, bk_sb = sb("bq_sb", [P, 2]), sb("bk_sb", [P, 2])
    bv_sb, bo_sb = sb("bv_sb", [P, D]), sb("bo_sb", [P, D])
    minus_half = sb("minus_half", [P, HT])
    heads_sb, heads_bf = sb("heads_sb", [P, KEYS_W]), sb("heads_bf", [P, KEYS_W], BF16)
    peaks = sb("peaks", [P, 4])
    norms = sb("norms", [1, P])
    terms = sb("terms", [1, KEYS_W + 2 * P + 1])
    bound = sb("bound", [1, NB])
    xin, xn, z = (sb(n, [P, HT, D]) for n in ("xin", "xn", "z"))
    stats = sb("stats", [P, HT, 6])
    mv1, mv2 = sb("mv1", [P, HT, 2]), sb("mv2", [P, HT, 2])
    ve1, ve2 = sb("ve1", [P, HT]), sb("ve2", [P, HT])
    rstd1, rstd2 = sb("rstd1", [P, HT]), sb("rstd2", [P, HT])
    xnT = sb("xnT", [P, DC, HALF])
    znT = sb("znT", [P, DC, HALF])
    zn_hi, zn_lo = sb("zn_hi", [P, DC, S], F32R), sb("zn_lo", [P, DC, S], F32R)
    lg_max, lg_sum, lg_rec = (sb(n, [P, HT]) for n in ("lg_max", "lg_sum", "lg_rec"))
    lg, lg_exp = sb("lg", [P, HT, E]), sb("lg_exp", [P, HT, E])
    qk = [sb(f"qk{i}", [P, HALF]) for i in range(4)]
    rot = [sb(f"rot{i}", [P, HALF]) for i in range(4)]
    square = [sb(f"square{i}", [P, HALF], BF16) for i in range(4)]
    parts = [sb(f"parts{i}", [P, NPART, 2, HALF], BF16) for i in range(2)]
    v_sb = sb("v_sb", [P, KT, D])
    q_stack = [sb(f"q_stack{i}", [P, HPG, S], BF16) for i in range(2)]
    k_stack = [sb(f"k_stack{i}", [P, HPG, S], BF16) for i in range(2)]
    v_ones = [sb(f"v_ones{i}", [P, KT, HPG, KEYS_W]) for i in range(2)]
    probs = [sb(f"probs{i}", [P, HPG, HALF]) for i in range(3)]
    row_max = sb("row_max", [P, HPG * KT])
    neg_max, neg_rest = sb("neg_max", [HPG * KT, P]), sb("neg_rest", [HPG * KT, P])
    shift = sb("shift", [HPG * KT, NPART, P], BF16)
    o_sb = [sb(f"o_sb{i}", [P, HALF]) for i in range(2)]
    num, rec = sb("num", [P, DC, HALF]), sb("rec", [P, DC, HALF])
    den, den_rec = sb("den", [P, NHEAD * HALF // P]), sb("den_rec", [P, NHEAD * HALF // P])
    at_hi = [sb(f"at_hi{i}", [P, DC, 2 * P], F32R) for i in range(2)]
    at_lo = [sb(f"at_lo{i}", [P, DC, 2 * P], F32R) for i in range(2)]
    base = sb("base", [P, TT, D])
    top_scores = znT[0:BE, :, :].rearrange("p c n -> p (c n)")

    score = [ps(f"score{i}", [P, 2, HALF]) for i in range(2)]
    o_ps = ps("o_ps", [P, HALF])
    wo_ps = ps("wo_ps", [P, 2, D])
    side = [ps(f"side{i}", [P, HALF]) for i in range(2)]

    const_in, weights_in = sem("const_in"), sem("weights_in")
    ones_set, zeros_set, heads_set, passed = sem("ones_set"), sem("zeros_set"), sem("heads_set"), sem("passed")
    const_set, weights_split, weights_high = sem("const_set"), sem("weights_split"), sem("weights_high")
    x_in, base_out, xn_out = sem("x_in"), sem("base_out"), sem("xn_out")
    stats1_done, stats2_done, rstd1_done, rstd2_done = (
        sem(n) for n in ("stats1_done", "stats2_done", "rstd1_done", "rstd2_done"))
    xn_ready, z_ready = sem("xn_ready"), sem("z_ready")
    side_full, side_free = sem("side_full"), sem("side_free")
    zn_ready, lg_exped, aff_done = sem("zn_ready"), sem("lg_exped"), sem("aff_done")
    parts_ready, parts_out = sem("parts_ready"), sem("parts_out")
    v_ones_ready = sem("v_ones_ready")
    stack_in = [sem(f"stack_in{i}") for i in range(2)]
    max_full, max_free, max_turned = sem("max_full"), sem("max_free"), sem("max_turned")
    shift_ready, shift_out, shift_in = sem("shift_ready"), sem("shift_out"), sem("shift_in")
    qk_done = [sem(f"qk_done{i}") for i in range(2)]
    exp_done = [sem(f"exp_done{i}") for i in range(2)]
    pv_done, o_copied = sem("pv_done"), sem("o_copied")
    o_out = [sem(f"o_out{i}") for i in range(2)]
    den_in, den_done, rec_out = sem("den_in"), sem("den_done"), sem("rec_out")
    sums_in, base_in, y_out = sem("sums_in"), sem("base_in"), sem("y_out")
    at_split, wo_done, y_ready = sem("at_split"), sem("wo_done"), sem("y_ready")
    aff_turned, top_copied = sem("aff_turned"), sem("top_copied")
    dve_n = Tally(sem("dve_n"), 2)
    dve_a = Tally(sem("dve_a"), 14)
    dve_b = Tally(sem("dve_b"), 4)
    dve_f = Tally(sem("dve_f"), 3)
    rotated, divided, sq_ready, v_peaked, bound_ready = (sem(n) for n in ("rotated", "divided", "sq_ready", "v_peaked", "bound_ready"))
    dve_d = Tally(sem("dve_d"), 4)
    dve_t = Tally(sem("dve_t"), 3 * CAP // 8)
    pool_a = Tally(sem("pool_a"), 4)

    HPC = P // HD
    CONSTS = 12
    JOB = ((0, 1, 2, 3, 4, 5, 6, 7, 8, 13), (9, 10, 11, 12, 14, 15, 16, 17, 18, 22))
    VJOB = (19, 20, 21, 23)
    V_AFTER = {(1, 8): (0, 1, 2), (1, 9): (3,)}
    PJOB = 24
    JOBS = PJOB + 2
    HJOBS = len(JOB[0])
    LIMIT = (SCORE_LIMIT / SCALE) ** 2
    LIMIT_BITS = int(np.float32(LIMIT).view(np.int32))
    QUARTERS = S // (2 * P)
    PARTS_DMA = 2 * DMA
    STACK_DMA = 2 * len(RUNS) * DMA

    HALF_STEPS = (((5, 6), (7, 8), (9, 10), (11, 12), (13, 14),
                   (15, 16, 17), (18, 19, 20), (21, 22, 23), (24, 25, 26), (35, 36)),
                  ((27, 28), (29, 30), (31, 32), (33, 34), (37, 38),
                   (39, 40, 41), (42, 43, 44), (45, 46, 47), (48, 49, 50), (56, 57)))
    V_STEPS = ((51, 51, 52), (52, 53, 53), (54, 54, 55), (57, 58, 58))
    PEAK_STEP = (60, 61)
    EXTRA_STEP = 54
    assert EXTRA_STEP % 3 == 0 and (STEPS - 1) % 3 == 0
    WO_STEPS = ((11, 12, 13), (14, 15, 16), (40, 41, 42), (43, 44, 45))
    NORM_STEP, ROUTER_STEP, AFFINITY_STEP = (2, 15), (15, 39), (18, 42)
    ROTARY_STEP, PARTS_STEP = ((21, 26), (45, 50)), ((25, 29), (46, 51))
    DEN_STEP, SPLIT_STEP = (3, 24), (9, 35)
    TOP_OPS = 3 * CAP // 8

    raw_weights = [probs[0][:, i, :].rearrange("p (c n) -> p c n", c=DC) for i in range(4)]

    def in_order():
        return sorted(((th, k) for th in range(2) for k in range(HJOBS)), key=lambda tk: JOB[tk[0]][tk[1]])

    def probs_of(s):
        return s % 3 if s < EXTRA_STEP else 1 if s == EXTRA_STEP else (s - EXTRA_STEP - 1) % 3

    def steps_since(s):
        return next(n for n in range(1, STEPS) if probs_of((s - n) % STEPS) == probs_of(s))

    def need(eng, s, value):
        if not isinstance(value, int) or value > 0:
            eng.wait_ge(s, value)

    def hold(eng, s, value):
        need(eng, s, value)
        if not isinstance(value, int):
            eng.sem_inc(passed, 1)

    def scores_wide(eng, b):
        hold(eng, bound_ready, b + 1)
        bits = bound[0:1, b:b + 1] if isinstance(b, int) else bound[0:1, bass.ds(b, 1)]
        return eng.value_load(bits.bitcast(mybir.dt.int32), min_val=0, max_val=2 ** 31 - 1) > LIMIT_BITS

    def passes_on(eng, *counts):
        for s, n in counts:
            eng.sem_inc(s, n)

    block = ctx.enter_context(nc.Block())

    @block.sync
    def _(sp):
        consts = ((ident_sb[:, :], g["ident"]), (row0_sb[:, :], g["row0"]),
                  (cos_sb[:, :], g["cos"]), (sin_sb[:, :], g["sin"]),
                  (gate_sb[:, :, :], g["gate_w"].rearrange("(c p) e -> p c e", p=P)),
                  (heads_sb[:, :], g["heads"]),
                  (lnw_sb[:, :], g["ln_w"]),
                  (lnb_sb[:, :], g["ln_b"]),
                  (bq_sb[:, :], g["bq"]),
                  (bk_sb[:, :], g["bk"]),
                  (bv_sb[:, :], g["bv"].partition_broadcast(P)),
                  (bo_sb[:, :], g["bo"].partition_broadcast(P)))
        assert len(consts) == CONSTS
        for i, name in enumerate(("wq_t", "wk_t", "wv_t", "wo_t")):
            sp.dma_start(raw_weights[i], g[name].rearrange("(c p) n -> p c n", p=P)).then_inc(weights_in, DMA)
        for to, of in consts:
            sp.dma_start(to, of).then_inc(const_in, DMA)

        def load_stack(b, hg):
            par, heads, r = hg % 2, slice(hg * HPG, (hg + 1) * HPG), 0
            for part, n in enumerate(RUNS):
                rows = slice(r * HD, (r + n) * HD)
                sp.dma_start(q_stack[par][rows, :, :].rearrange("c h n -> c (h n)"),
                             q_dram[b, part, :, :, heads].rearrange("a i h n -> (a i) (h n)")
                             .unsqueeze(0).to_broadcast([n, HD, HPG * S])).then_inc(stack_in[par], DMA)
                sp.dma_start(k_stack[par][rows, :, :].rearrange("c h n -> c (h n)"),
                             k_dram[b, 0:n, :, :, heads].rearrange("p a i h n -> (p a i) (h n)"))\
                  .then_inc(stack_in[par], DMA)
                r += n

        def store_parts(n, th):
            hold(sp, parts_ready, 2 * n + th + 1)
            for src, dram in ((0, q_dram), (1, k_dram)):
                sp.dma_start(dram[n, :, :, :, :, th * HALF:(th + 1) * HALF].rearrange("p a i h n -> (i h) (p a) n"),
                             parts[src][:, :, :, :].rearrange("k p a n -> k (p a) n")).then_inc(parts_out, DMA)

        def shift_rows(b, hg, wide):
            u = b * NG + hg
            with sp.If(wide):
                hold(sp, shift_ready, u + 1)
                sp.dma_start(shift_dram[b, hg].rearrange("c t n -> t c n"), shift[:, :, :])\
                  .then_inc(shift_out, DMA)
                hold(sp, shift_out, DMA * (u + 1))
                sp.dma_start(q_stack[hg % 2][SHIFT:FULL, :, :].rearrange("c h n -> c (h n)"),
                             shift_dram[b, hg].rearrange("c t n -> c (t n)")).then_inc(shift_in, DMA)
            with sp.Else():
                passes_on(sp, (shift_out, DMA), (shift_in, DMA))

        def store_o(b, il):
            i = b * 2 * NG + il
            hold(sp, o_copied, i + 1)
            sp.dma_start(o_dram[b, il % 2, il // 2].rearrange("j w r n -> (j w r) n"),
                         o_sb[il % 2][:, :]).then_inc(o_out[il % 2], DMA)

        def load_sums(d, qh):
            hold(sp, o_out[qh], DMA * NG * (d + 1))
            eighths = P // NHEAD
            sp.dma_start(den[:, :], o_dram[d, qh, :, :, 1, 0, :].rearrange("g j (c n) -> (g j) c n", c=eighths))\
              .then_inc(den_in, DMA)
            if qh == 1:
                hold(sp, at_split, QUARTERS * d + QUARTERS // 2)
            for c in range(DC):
                sp.dma_start(num[:, c, :], o_dram[d, qh, 2 * c:2 * c + 2, :, 0].rearrange("g j r n -> (g j) r n"))\
                  .then_inc(sums_in, DMA)

        def load_base(d):
            hold(sp, base_out, 2 * DMA * (d + 1))
            rows = out[bass.ds(d * S, S), :].rearrange("(t p) n -> p t n", p=P)
            sp.dma_start(base[:, :, :], rows).then_inc(base_in, DMA)

        def spread_rec(d, qh):
            hold(sp, den_done, 2 * d + qh + 1)
            sp.dma_start(rec_dram[d, qh].rearrange("h (c n) -> (h c) n", c=P // NHEAD), den_rec[:, :])\
              .then_inc(rec_out, DMA)
            hold(sp, rec_out, DMA * (2 * d + qh + 1))
            for c in range(DC):
                src = rec_dram[d, qh, c * HPC:(c + 1) * HPC].unsqueeze(1).to_broadcast([HPC, HD, HALF])
                sp.dma_start(rec[:, c, :], src).then_inc(sums_in, DMA)

        def store_y(d):
            rows = out[bass.ds(d * S, S), :].rearrange("(t p) n -> p t n", p=P)
            for hf in range(2):
                hold(sp, y_ready, QUARTERS * d + 2 * hf + 2)
                sp.dma_start(rows[:, hf * HT:(hf + 1) * HT, :], base[:, hf * HT:(hf + 1) * HT, :])\
                  .then_inc(y_out, DMA)

        def first_stack(n):
            hold(sp, parts_out, (n + 1) * 2 * PARTS_DMA)
            load_stack(n, 0)

        def attend(b, nxt, prev):
            wide = scores_wide(sp, b)
            hold(sp, exp_done[1], b * STEPS)
            load_stack(b, 1)
            shift_rows(b, 0, wide)
            if prev is not None:
                store_o(prev, 2 * NG - 1)
                load_sums(prev, 0)
                load_base(prev)
                spread_rec(prev, 0)
            store_o(b, 0)
            hold(sp, exp_done[1], b * STEPS + 2 * KT)
            shift_rows(b, 1, wide)
            load_stack(b, 2)
            store_o(b, 1)
            if prev is not None:
                load_sums(prev, 1)
                spread_rec(prev, 1)
            store_o(b, 2)
            if nxt is not None:
                store_parts(nxt, 0)
            hold(sp, exp_done[1], b * STEPS + 4 * KT)
            shift_rows(b, 2, wide)
            load_stack(b, 3)
            store_o(b, 3)
            store_o(b, 4)
            if prev is not None:
                store_y(prev)
                hold(sp, y_out, 2 * DMA * (prev + 1))
            hold(sp, exp_done[1], b * STEPS + 6 * KT)
            shift_rows(b, 3, wide)
            store_o(b, 5)
            if nxt is not None:
                store_parts(nxt, 1)
                first_stack(nxt)
            store_o(b, 6)

        store_parts(0, 0)
        store_parts(0, 1)
        first_stack(0)
        attend(0, 1, None)
        with sp.Fori(1, NB - 1) as b:
            attend(b, b + 1, b - 1)
        attend(NB - 1, None, NB - 2)
        load_sums(NB - 1, 0)
        load_base(NB - 1)
        spread_rec(NB - 1, 0)
        store_o(NB - 1, 2 * NG - 1)
        load_sums(NB - 1, 1)
        spread_rec(NB - 1, 1)
        store_y(NB - 1)
        hold(sp, y_out, 2 * DMA * NB)

    @block.gpsimd
    def _(pool):
        pool.dma_start(xin[:, :, :], x[0:HALF, :].rearrange("(t p) n -> p t n", p=P)).then_inc(x_in, DMA)
        pool.memset(minus_half[:, :], -0.5).then_inc(const_set, 1)
        for i in range(2):
            pool.memset(v_ones[i][:, :, :, :], 1.0).then_inc(const_set, 1)

        def load_x(n, th):
            hold(pool, base_out, DMA * (2 * n + th))
            pool.dma_start(xin[:, :, :], x[bass.ds(n * S + th * HALF, HALF), :]
                           .rearrange("(t p) n -> p t n", p=P)).then_inc(x_in, DMA)

        def deviations(n, th):
            u = 2 * n + th
            pool_a.start(u)
            for stats_done, mv, ve, rstd, rstd_done in ((stats1_done, mv1, ve1, rstd1, rstd1_done),
                                                        (stats2_done, mv2, ve2, rstd2, rstd2_done)):
                hold(pool, stats_done, u + 1)
                pool_a.mark(pool.tensor_scalar(ve[:, :], mv[:, :, 1], LN_EPS, None, ALU.add))
                pool_a.settle(pool, hold)
                pool.tensor_tensor(rstd[:, :], ve[:, :], minus_half[:, :], ALU.pow).then_inc(rstd_done, 1)

        def base_rows(n, th):
            out_rows = xn_dram[bass.ds(n * S + th * HALF, HALF), :].rearrange("(t p) n -> p t n", p=P)
            pool.dma_start(out_rows, xn[:, :, :]).then_inc(xn_out, DMA)
            pool_a.mark(pool.tensor_tensor(xin[:, :, :], xin[:, :, :], xn[:, :, :], ALU.add))
            pool_a.settle(pool, hold)
            for t in range(HT):
                last = pool.tensor_tensor(xin[:, t, :], xin[:, t, :], bo_sb[:, :], ALU.add)
            pool_a.mark(last)
            pool_a.settle(pool, hold)
            to = out[bass.ds(n * S + th * HALF, HALF), :].rearrange("(t p) n -> p t n", p=P)
            pool.dma_start(to, xin[:, :, :]).then_inc(base_out, DMA)
            pool_a.end()

        def set_v(b, hg):
            hold(pool, pv_done, (b * NG + hg - 1) * 2 * KT)
            pool.tensor_copy(v_ones[hg % 2][:, :, :, 0:HD],
                             v_sb[:, :, hg * HPG * HD:(hg + 1) * HPG * HD]
                             .rearrange("p t (j d) -> p t j d", j=HPG)).then_inc(v_ones_ready, 1)

        def squares(n, th):
            hold(pool, rotated, 2 * n + th + 1)
            for i in range(4):
                last = pool.tensor_tensor(square[i][:, :], qk[i][:, :], qk[i][:, :], ALU.mult)
            last.then_inc(sq_ready, 1)

        def divide(d, qh):
            hold(pool, sums_in, (2 * d + qh + 1) * 2 * DC * DMA)
            pool.tensor_tensor(num[:, :, :], num[:, :, :], rec[:, :, :], ALU.mult).then_inc(divided, 1)

        def attend(b, nxt, prev):
            if nxt is not None:
                load_x(nxt, 0)
            set_v(b, 1)
            if nxt is not None:
                deviations(nxt, 0)
            if prev is not None:
                divide(prev, 0)
            if nxt is not None:
                base_rows(nxt, 0)
                load_x(nxt, 1)
            set_v(b, 2)
            if nxt is not None:
                deviations(nxt, 1)
                squares(nxt, 0)
                base_rows(nxt, 1)
            if prev is not None:
                divide(prev, 1)
            set_v(b, 3)
            if nxt is not None:
                squares(nxt, 1)
                hold(pool, side_free, nxt * JOBS + PJOB)
                set_v(nxt, 0)

        hold(pool, const_set, 3)
        deviations(0, 0)
        hold(pool, const_in, CONSTS * DMA)
        base_rows(0, 0)
        load_x(0, 1)
        deviations(0, 1)
        base_rows(0, 1)
        squares(0, 0)
        squares(0, 1)
        hold(pool, side_free, PJOB)
        set_v(0, 0)
        attend(0, 1, None)
        with pool.Fori(1, NB - 1) as b:
            attend(b, b + 1, b - 1)
        attend(NB - 1, None, NB - 2)
        divide(NB - 1, 0)
        divide(NB - 1, 1)
        hold(pool, base_out, 2 * DMA * NB)
        hold(pool, xn_out, 2 * DMA * NB)

    @block.scalar
    def _(act):
        def router(n, th):
            act.wait_ge(side_free, n * JOBS + JOB[th][4] + 1)
            act.activation(lg_exp[:, :, :], lg[:, :, :], ACT.Exp).then_inc(lg_exped, 1)

        def attend(b, nxt, prev):
            for s in range(STEPS):
                at = b * STEPS + s
                for i in range(2):
                    act.wait_ge(qk_done[i], at + 1)
                    if i == 0:
                        need(act, pv_done, at - steps_since(s) + 1)
                    act.activation(probs[probs_of(s)][:, 2 * i:2 * i + 2, :], score[i][:, :, :], ACT.Exp,
                                   scale=SCALE).then_inc(exp_done[i], 1)
                if nxt is not None and s in ROUTER_STEP:
                    router(nxt, ROUTER_STEP.index(s))

        act.wait_ge(weights_in, 4 * DMA)
        for i in range(4):
            act.copy(w_hi[i][:, :, :], raw_weights[i]).then_inc(weights_high, 1)
        router(0, 0)
        router(0, 1)
        act.wait_ge(weights_split, 1)
        attend(0, 1, None)
        with act.Fori(1, NB - 1) as b:
            attend(b, b + 1, b - 1)
        attend(NB - 1, None, NB - 2)

    @block.tensor
    def _(pe):
        def open_side(n, job):
            need(pe, side_free, n * JOBS + job - 1)
            return side[job % 2]

        def half_job(n, th, k, piece):
            u, job = 2 * n + th, JOB[th][k]
            cols = slice(th * HALF, (th + 1) * HALF)
            bank = open_side(n, job) if piece == 0 else side[job % 2]
            if k < 4:
                src, ready, c = ((xn, xn_ready), (z, z_ready))[k // 2] + (k % 2,)
                pe.wait_ge(ready, u + 1)
                for t in range(piece * HT // 2, (piece + 1) * HT // 2):
                    last = pe.transpose(bank[:, t * P:(t + 1) * P], src[:, t, c * P:(c + 1) * P], ident_sb[:, :])
            elif k == 4:
                for t in range(piece * HT // 2, (piece + 1) * HT // 2):
                    for c in range(DC):
                        last = pe.matmul(bank[:, t * E:(t + 1) * E], xnT[:, c, t * P:(t + 1) * P],
                                         gate_sb[:, c, :], start=c == 0, stop=c == DC - 1)
            elif k == 9:
                pe.wait_ge(sq_ready, u + 1)
                for a in range(2):
                    last = pe.matmul(bank[piece * KEYS_W:(piece + 1) * KEYS_W, :], heads_bf[:, :],
                                     square[2 * piece + a][:, :], start=a == 0, stop=a == 1)
            else:
                w, a = ((WQ, 0), (WQ, 1), (WK, 0), (WK, 1))[k - 5]
                pe.wait_ge(zn_ready, u + 1)
                wt, zt = PASSES(w)[piece]
                for c in range(DC):
                    last = pe.matmul(bank[:, :], wt[:, c, a * P:(a + 1) * P], zt[:, c, cols],
                                     start=piece == 0 and c == 0, stop=piece == 2 and c == DC - 1)
            if piece == len(HALF_STEPS[th][k]) - 1:
                last.then_inc(side_full, 1)

        TILE_PASSES = (((0, 0), (0, 1)), ((0, 2), (1, 0)), ((1, 1), (1, 2)))

        def PASSES(w):
            return (w_hi[w], zn_hi), (w_lo[w], zn_hi), (w_hi[w], zn_lo)

        def v_job(n, pair, piece):
            job = VJOB[pair]
            bank = open_side(n, job) if piece == 0 else side[job % 2]
            pe.wait_ge(zn_ready, 2 * n + 2)
            for t2, i in TILE_PASSES[piece]:
                t, (wt, zt) = 2 * pair + t2, PASSES(WV)[i]
                for c in range(DC):
                    last = pe.matmul(bank[:, t2 * D:(t2 + 1) * D], zt[:, c, t * P:(t + 1) * P], wt[:, c, :],
                                     start=i == 0 and c == 0, stop=i == 2 and c == DC - 1)
            if piece == 2:
                last.then_inc(side_full, 1)

        def peak_job(n, i):
            bank = open_side(n, PJOB + i)
            if i == 0:
                pe.wait_ge(side_free, n * JOBS + PJOB)
            else:
                pe.wait_ge(v_peaked, n + 1)
            for c in range(2):
                last = pe.transpose(bank[0:1, c * P:(c + 1) * P], peaks[:, 2 * i + c:2 * i + c + 1], ident_sb[:, :])
            last.then_inc(side_full, 1)

        def wo_job(d, quarter, piece):
            pe.wait_ge(at_split, QUARTERS * d + quarter + 1)
            if piece == 0 and quarter > 0:
                pe.wait_ge(y_ready, QUARTERS * d + quarter)
            hi, lo = at_hi[quarter % 2], at_lo[quarter % 2]
            for t, i in TILE_PASSES[piece]:
                at, wt = ((hi, w_hi[WO]), (lo, w_hi[WO]), (hi, w_lo[WO]))[i]
                for c in range(DC):
                    last = pe.matmul(wo_ps[:, t, :], at[:, c, t * P:(t + 1) * P], wt[:, c, :],
                                     start=i == 0 and c == 0, stop=i == 2 and c == DC - 1)
            if piece == 2:
                last.then_inc(wo_done, 1)

        def maxima(b, hg, at):
            u, n = b * NG + hg, HPG * KT
            par = hg % 2
            for i in range(2):
                need(pe, exp_done[i], at)
            for k in range(n):
                j, t = k // KT, k % KT
                if k >= 2:
                    pe.wait_ge(max_free, u * n + k - 1)
                for kh in range(2):
                    last = pe.matmul(score[k % 2][:, kh, :], q_stack[par][0:ROWS, j, t * P:(t + 1) * P],
                                     k_stack[par][0:ROWS, j, kh * HALF:(kh + 1) * HALF], start=True, stop=True)
                last.then_inc(max_full, 1)
            pe.wait_ge(max_free, u * n + n)
            pe.transpose(score[0][0:n, 0, 0:P], row_max[:, :], ident_sb[:, :]).then_inc(max_turned, 1)
            pe.wait_ge(shift_in, (u + 1) * DMA)

        def pv(s, done, g_half=None, group=None):
            par, kt = (s // (2 * KT)) % 2, s % KT
            for i in range(2):
                pe.wait_ge(exp_done[i], done)
            if kt == 0:
                need(pe, o_copied, g_half)
            if s % (2 * KT) == 0:
                pe.wait_ge(v_ones_ready, group + 1)
            for j in range(HPG):
                last = pe.matmul(o_ps[j * KEYS_W:(j + 1) * KEYS_W, :], v_ones[par][:, kt, j, :],
                                 probs[probs_of(s)][:, j, :], start=kt == 0, stop=kt == KT - 1)
            last.then_inc(pv_done, 1)

        def turn_affinities():
            pe.wait_ge(aff_done, 2 * NB)
            pe.wait_ge(side_free, NB * JOBS)
            for t in range(TT):
                last = pe.transpose(side[t // HT][0:BE, (t % HT) * P:(t % HT + 1) * P], affinity[:, t, :],
                                    ident_sb[:, :])
            last.then_inc(aff_turned, 1)

        def attend(b, nxt, prev):
            wide = scores_wide(pe, b)
            for s in range(STEPS):
                at = b * STEPS + s
                hg, par, qh, kt = s // (2 * KT), (s // (2 * KT)) % 2, (s // KT) % 2, s % KT
                if s % (2 * KT) == 0:
                    pe.wait_ge(stack_in[par], (b * (NG // 2) + hg // 2 + 1) * STACK_DMA)
                    with pe.If(wide):
                        maxima(b, hg, at)
                    with pe.Else():
                        passes_on(pe, (max_full, HPG * KT), (max_turned, 1))
                for i in range(2):
                    need(pe, exp_done[i], at)
                    for j in range(2):
                        last = pe.matmul(score[i][:, j, :], k_stack[par][0:FULL, 2 * i + j, kt * P:(kt + 1) * P],
                                         q_stack[par][0:FULL, 2 * i + j, qh * HALF:(qh + 1) * HALF],
                                         start=True, stop=True)
                    last.then_inc(qk_done[i], 1)
                    if i == 0 and s >= 2:
                        pv(s - 2, at - 1, b * 2 * NG + (s - 2) // KT, b * NG + (s - 2) // (2 * KT))
                    elif i == 0 and (not isinstance(b, int) or b > 0):
                        pv(s - 2 + STEPS, at - 1)
                if prev is not None:
                    for quarter in range(QUARTERS):
                        for piece, at_step in enumerate(WO_STEPS[quarter]):
                            if at_step == s:
                                wo_job(prev, quarter, piece)
                if nxt is not None:
                    for th in range(2):
                        for k in range(HJOBS):
                            for piece, at_step in enumerate(HALF_STEPS[th][k]):
                                if at_step == s:
                                    half_job(nxt, th, k, piece)
                    for pair in range(KT // 2):
                        for piece, at_step in enumerate(V_STEPS[pair]):
                            if at_step == s:
                                v_job(nxt, pair, piece)
                    if s in PEAK_STEP:
                        peak_job(nxt, PEAK_STEP.index(s))
                elif s == 0:
                    turn_affinities()

        pe.wait_ge(const_in, CONSTS * DMA)
        pe.wait_ge(weights_split, 1)
        pe.wait_ge(const_set, 3)
        pe.wait_ge(ones_set, 4)
        pe.wait_ge(heads_set, 1)
        pe.wait_ge(zeros_set, 2)
        for th, k in in_order():
            for piece in range(len(HALF_STEPS[th][k])):
                half_job(0, th, k, piece)
            for pair in V_AFTER.get((th, k), ()):
                for piece in range(3):
                    v_job(0, pair, piece)
        for i in range(2):
            peak_job(0, i)
        attend(0, 1, None)
        with pe.Fori(1, NB - 1) as b:
            attend(b, b + 1, b - 1)
        attend(NB - 1, None, NB - 2)
        for s in (STEPS - 2, STEPS - 1):
            pv(s, (NB - 1) * STEPS + s + 1)
        for quarter in range(QUARTERS):
            for piece in range(3):
                wo_job(NB - 1, quarter, piece)

    @block.vector
    def _(dve):
        def stats_of(n, src, mv, done):
            for t in range(HT):
                last = dve.bn_stats(stats[:, t, :], src[:, t, :])
            dve_n.mark(last)
            dve_n.settle(dve, hold)
            for t in range(HT):
                last = dve.bn_aggr(mv[:, t, :], stats[:, t, :])
            last.then_inc(done, 1)

        def scaled(to, src, mv, rstd, ready=None):
            for t in range(HT):
                last = dve.tensor_scalar(to[:, t, :], src[:, t, :], mv[:, t, 0:1], rstd[:, t:t + 1],
                                         ALU.subtract, ALU.mult)
            last.then_inc(ready, 1)

        def norm1(n, th):
            u = 2 * n + th
            dve_n.start(u)
            dve.wait_ge(x_in, DMA * (u + 1))
            stats_of(n, xin, mv1, stats1_done)

        def norm2(n, th):
            u = 2 * n + th
            dve.wait_ge(rstd1_done, u + 1)
            need(dve, xn_out, DMA * u)
            scaled(xn, xin, mv1, rstd1, xn_ready)
            dve.wait_ge(xn_ready, u + 1)
            stats_of(n, xn, mv2, stats2_done)

        def norm3(n, th):
            dve.wait_ge(rstd2_done, 2 * n + th + 1)
            scaled(z, xn, mv2, rstd2, z_ready)
            dve_n.end()

        def take(n, job):
            dve.wait_ge(side_full, n * JOBS + job + 1)
            return side[job % 2]

        def turned_x(n, th, c):
            job = JOB[th][c]
            bank = take(n, job)
            dve.tensor_copy(xnT[:, c, :], bank[:, :]).then_inc(side_free, 1)

        def turned_z(n, th, c):
            bank = take(n, JOB[th][2 + c])
            dve.tensor_scalar(znT[:, c, :], bank[:, :], lnw_sb[:, c:c + 1], lnb_sb[:, c:c + 1],
                              ALU.mult, ALU.add).then_inc(side_free, 1)
            if c == DC - 1:
                cols = slice(th * HALF, (th + 1) * HALF)
                dve_a.start(2 * n + th)
                dve.wait_ge(side_free, n * JOBS + JOB[th][3] + 1)
                dve_a.mark(dve.tensor_copy(zn_hi[:, :, cols], znT[:, :, :]))
                dve_a.settle(dve)
                dve.tensor_tensor(zn_lo[:, :, cols], znT[:, :, :], zn_hi[:, :, cols], ALU.subtract)\
                   .then_inc(zn_ready, 1)

        def logits(n, th):
            bank = take(n, JOB[th][4])
            view = bank[:, 0:HT * E].rearrange("p (t e) -> p t e", e=E)
            dve_a.mark(dve.tensor_reduce(lg_max[:, :], view, AX_X, ALU.max))
            dve_a.settle(dve)
            dve.tensor_tensor(lg[:, :, :], view, lg_max[:, :].unsqueeze(2).to_broadcast([P, HT, E]),
                              ALU.subtract).then_inc(side_free, 1)

        def affinities(n, th):
            u = 2 * n + th
            dve.wait_ge(lg_exped, u + 1)
            dve_a.mark(dve.tensor_reduce(lg_sum[:, :], lg_exp[:, :, :], AX_X, ALU.add))
            dve_a.settle(dve)
            dve_a.mark(dve.reciprocal(lg_rec[:, :], lg_sum[:, :]))
            dve_a.settle(dve)
            for t in range(HT):
                last = dve.tensor_scalar(affinity[:, th * HT + t, bass.ds(n * E, E)], lg_exp[:, t, :],
                                         lg_rec[:, t:t + 1], None, ALU.mult)
            last.then_inc(aff_done, 1)

        def biased(n, th, k):
            bank = take(n, JOB[th][5 + k])
            bias = (bq_sb, bk_sb)[k // 2]
            dve.tensor_scalar(qk[k][:, :], bank[:, :], bias[:, k % 2:k % 2 + 1], None, ALU.add)\
               .then_inc(side_free, 1)

        def rotary(n, th, s):
            cols = slice(th * HALF, (th + 1) * HALF)
            dve.wait_ge(side_free, n * JOBS + JOB[th][6 + 2 * s] + 1)
            a, b, t = qk[2 * s], qk[2 * s + 1], rot
            for i, (v, tab) in enumerate(((a, cos_sb), (b, sin_sb), (a, sin_sb), (b, cos_sb))):
                last = dve.tensor_tensor(t[i][:, :], v[:, :], tab[:, cols], ALU.mult)
            dve_a.mark(last)
            dve_a.settle(dve)
            dve.tensor_tensor(a[:, :], t[0][:, :], t[1][:, :], ALU.subtract)
            last = dve.tensor_tensor(b[:, :], t[2][:, :], t[3][:, :], ALU.add)
            if s == 0:
                dve_a.mark(last)
            else:
                last.then_inc(rotated, 1)

        def norm_peaks(n, th):
            bank = take(n, JOB[th][9])
            dve.tensor_reduce(peaks[0:2 * KEYS_W, th:th + 1], bank[0:2 * KEYS_W, :], AX_X, ALU.max)\
               .then_inc(side_free, 1)

        def value_peaks(n):
            dve.wait_ge(side_free, n * JOBS + PJOB)
            for i, op in enumerate((ALU.max, ALU.min)):
                last = dve.tensor_reduce(peaks[:, 2 + i:3 + i], v_sb[:, :, :].rearrange("p t d -> p (t d)"), AX_X, op)
            last.then_inc(v_peaked, 1)

        def limits(n):
            dve_f.start(n)
            bank = take(n, PJOB)
            dve.tensor_reduce(norms[:, :], bank[0:1, 0:2 * P].rearrange("o (h c) -> o c h", h=2), AX_X, ALU.max)\
               .then_inc(side_free, 1)
            bank = take(n, PJOB + 1)
            dve.tensor_scalar(terms[:, KEYS_W:KEYS_W + P], bank[0:1, 0:P], LIMIT / VALUE_LIMIT, None, ALU.mult)
            dve.tensor_scalar(terms[:, KEYS_W + P:KEYS_W + 2 * P], bank[0:1, P:2 * P], -LIMIT / VALUE_LIMIT, None,
                              ALU.mult).then_inc(side_free, 1)
            dve.wait_ge(side_free, (n + 1) * JOBS)
            dve_f.mark(dve.tensor_tensor(terms[:, 0:KEYS_W], norms[:, 0:KEYS_W], norms[:, KEYS_W:2 * KEYS_W], ALU.mult))
            dve_f.settle(dve)
            to = bound[:, n:n + 1] if isinstance(n, int) else bound[:, bass.ds(n, 1)]
            dve_f.mark(dve.tensor_reduce(to, terms[:, :], AX_X, ALU.max))
            dve_f.settle(dve, hold)
            dve_f.mark(dve.tensor_copy(terms[:, KEYS_W + 2 * P:], to))
            dve_f.settle(dve)
            dve.sem_inc(bound_ready, 1)
            dve_f.end()

        def split(n, th, s):
            u = 2 * n + th
            if s == 0:
                need(dve, parts_out, u * PARTS_DMA)
                dve_a.settle(dve)
            else:
                dve.wait_ge(rotated, u + 1)
            to, rest = parts[s], rot[2 * s:2 * s + 2]
            for i in range(2):
                last = dve.tensor_copy(to[:, 0, i, :], qk[2 * s + i][:, :])
            dve_a.mark(last)
            dve_a.settle(dve)
            for i in range(2):
                last = dve.tensor_tensor(rest[i][:, :], qk[2 * s + i][:, :], to[:, 0, i, :], ALU.subtract)
            dve_a.mark(last)
            dve_a.settle(dve)
            for i in range(2):
                last = dve.tensor_copy(to[:, 1, i, :], rest[i][:, :])
            dve_a.mark(last)
            dve_a.settle(dve)
            for i in range(2):
                last = dve.tensor_tensor(to[:, 2, i, :], rest[i][:, :], to[:, 1, i, :], ALU.subtract)
            if s == 0:
                dve_a.mark(last)
            else:
                last.then_inc(parts_ready, 1)
                dve_a.end()

        def values(n, pair):
            bank = take(n, VJOB[pair])
            if pair == 0:
                need(dve, v_ones_ready, NG * n)
            for t in range(2):
                last = dve.tensor_tensor(v_sb[:, 2 * pair + t, :], bank[:, t * D:(t + 1) * D], bv_sb[:, :], ALU.add)
            last.then_inc(side_free, 1)

        def half_job(n, th, k):
            if k < 2:
                turned_x(n, th, k)
            elif k < 4:
                turned_z(n, th, k - 2)
            elif k == 4:
                logits(n, th)
            elif k == 9:
                norm_peaks(n, th)
            else:
                biased(n, th, k - 5)

        def copy_o(b, il):
            i = b * 2 * NG + il
            dve.wait_ge(pv_done, (i + 1) * KT)
            need(dve, o_out[il % 2], (b * NG + il // 2) * DMA)
            dve.tensor_copy(o_sb[il % 2][:, :], o_ps[:, :]).then_inc(o_copied, 1)


        def invert(d, qh):
            dve.wait_ge(den_in, (2 * d + qh + 1) * DMA)
            dve.reciprocal(den_rec[:, :], den[:, :]).then_inc(den_done, 1)

        def quarter_split(d, quarter):
            cols = slice(quarter % 2 * 2 * P, (quarter % 2 + 1) * 2 * P)
            if quarter == 0:
                dve_d.start(d)
                dve.wait_ge(base_in, (d + 1) * DMA)
            if quarter % 2 == 0:
                dve.wait_ge(divided, 2 * d + quarter // 2 + 1)
            dve_d.mark(dve.tensor_copy(at_hi[quarter % 2][:, :, :], num[:, :, cols]))
            dve_d.settle(dve)
            dve.tensor_tensor(at_lo[quarter % 2][:, :, :], num[:, :, cols], at_hi[quarter % 2][:, :, :],
                              ALU.subtract).then_inc(at_split, 1)
            if quarter == QUARTERS - 1:
                dve_d.end()

        def add_base(d, quarter):
            dve.wait_ge(wo_done, QUARTERS * d + quarter + 1)
            rows = base[:, 2 * quarter:2 * quarter + 2, :]
            dve.tensor_tensor(rows, wo_ps[:, :, :], rows, ALU.add).then_inc(y_ready, 1)

        def maxima(b, hg):
            u, n = b * NG + hg, HPG * KT
            dve_b.start(u)
            for k in range(n):
                dve.wait_ge(max_full, u * n + k + 1)
                dve.tensor_reduce(row_max[:, k:k + 1], score[k % 2][:, :, :].rearrange("p a n -> p (a n)"),
                                  AX_X, ALU.max).then_inc(max_free, 1)
            dve.wait_ge(max_turned, u + 1)
            need(dve, shift_out, DMA * u)
            dve_b.mark(dve.tensor_scalar(neg_max[:, :], score[0][0:n, 0, 0:P], -1.0, None, ALU.mult))
            dve_b.settle(dve)
            dve_b.mark(dve.tensor_copy(shift[:, 0, :], neg_max[:, :]))
            dve_b.settle(dve)
            dve_b.mark(dve.tensor_tensor(neg_rest[:, :], neg_max[:, :], shift[:, 0, :], ALU.subtract))
            dve_b.settle(dve)
            dve_b.mark(dve.tensor_copy(shift[:, 1, :], neg_rest[:, :]))
            dve_b.settle(dve)
            dve.tensor_tensor(shift[:, 2, :], neg_rest[:, :], shift[:, 1, :], ALU.subtract).then_inc(shift_ready, 1)
            dve_b.end()

        def affinities_in():
            dve.wait_ge(aff_turned, 1)
            for half in range(2):
                last = dve.tensor_copy(top_scores[:, half * HALF:(half + 1) * HALF], side[half][0:BE, :])
            last.then_inc(top_copied, 1)
            dve.wait_ge(top_copied, 1)
            dve_t.start(0)

        def take_top(op):
            eight = slice(8 * (op // 3), 8 * (op // 3) + 8)
            if op > 0:
                dve_t.settle(dve)
            if op % 3 == 0:
                dve_t.mark(dve.max(top_gate[:, eight], top_scores))
            elif op % 3 == 1:
                dve_t.mark(dve.max_index(top_row[:, eight], top_gate[:, eight], top_scores))
            else:
                dve_t.mark(dve.match_replace(top_scores, top_gate[:, eight], top_scores, -1.0))

        def attend(b, nxt, prev):
            wide = scores_wide(dve, b)
            for s in range(STEPS):
                if s % (2 * KT) == 0:
                    with dve.If(wide):
                        maxima(b, s // (2 * KT))
                    with dve.Else():
                        passes_on(dve, (max_free, HPG * KT), (dve_b.sem, dve_b.per), (shift_ready, 1))
                if s % KT == 1:
                    if s > 1:
                        copy_o(b, s // KT - 1)
                    elif prev is not None:
                        copy_o(prev, 2 * NG - 1)
                if prev is not None:
                    if s in DEN_STEP:
                        invert(prev, DEN_STEP.index(s))
                    if s in SPLIT_STEP:
                        for i in range(2):
                            quarter_split(prev, 2 * SPLIT_STEP.index(s) + i)
                    for quarter in range(QUARTERS):
                        if WO_STEPS[quarter][-1] == s:
                            add_base(prev, quarter)
                if nxt is not None:
                    for th, at in enumerate(NORM_STEP):
                        if s == at:
                            norm1(nxt, th)
                        if s == at + 2:
                            norm2(nxt, th)
                        if s == at + 4:
                            norm3(nxt, th)
                    for th, k in in_order():
                        if HALF_STEPS[th][k][-1] == s:
                            half_job(nxt, th, k)
                    for th in range(2):
                        if s == AFFINITY_STEP[th]:
                            affinities(nxt, th)
                        for i in range(2):
                            if s == ROTARY_STEP[th][i]:
                                rotary(nxt, th, i)
                            if s == PARTS_STEP[th][i]:
                                split(nxt, th, i)
                    for pair in range(KT // 2):
                        if V_STEPS[pair][-1] == s:
                            values(nxt, pair)
                    if s == V_STEPS[-1][-1]:
                        value_peaks(nxt)
                    if s == PEAK_STEP[-1]:
                        limits(nxt)
                else:
                    if s == 0:
                        affinities_in()
                    if s == STEPS - 2:
                        invert(b, 0)
                    for op in range(TOP_OPS * s // STEPS, TOP_OPS * (s + 1) // STEPS):
                        take_top(op)

        for i in range(2):
            dve.memset(k_stack[i][SHIFT:FULL, :, :], 1.0).then_inc(ones_set, 1)
            dve.memset(q_stack[i][SHIFT:FULL, :, :], 0.0).then_inc(ones_set, 1)
        dve.memset(peaks[:, :], 0.0).then_inc(zeros_set, 1)
        dve.memset(terms[:, :], 0.0).then_inc(zeros_set, 1)
        norm1(0, 0)
        dve.wait_ge(weights_high, 4)
        for i in range(4):
            last = dve.tensor_tensor(w_lo[i][:, :, :], raw_weights[i], w_hi[i][:, :, :], ALU.subtract)
        last.then_inc(weights_split, 1)
        norm2(0, 0)
        norm3(0, 0)
        dve.wait_ge(const_in, CONSTS * DMA)
        dve.tensor_copy(heads_bf[:, :], heads_sb[:, :]).then_inc(heads_set, 1)
        dve.wait_ge(zeros_set, 2)
        for th, k in in_order():
            half_job(0, th, k)
            for pair in V_AFTER.get((th, k), ()):
                values(0, pair)
            if k in (6, 8):
                s = (k - 6) // 2
                rotary(0, th, s)
                split(0, th, s)
            if k == 5:
                affinities(0, th)
            if th == 0 and k in (4, 5, 7):
                (norm1, norm2, norm3)[(k - 3) // 2](0, 1)
        value_peaks(0)
        limits(0)
        attend(0, 1, None)
        with dve.Fori(1, NB - 1) as b:
            attend(b, b + 1, b - 1)
        attend(NB - 1, None, NB - 2)
        copy_o(NB - 1, 2 * NG - 1)
        for qh in range(2):
            if qh == 1:
                invert(NB - 1, 1)
            for i in range(2):
                quarter_split(NB - 1, 2 * qh + i)
            for i in range(2):
                add_base(NB - 1, 2 * qh + i)


def expert_part(nc, ctx, g):
    (T, D, NB, S, DC, E, CAP, BE, F, FC) = (g[k] for k in "T D NB S DC E CAP BE F FC".split())
    out, xn_dram, wg, wu, wd = (g[k] for k in "out xn_dram wg wu wd".split())
    ident_sb, row0_sb, top_gate, top_row = (g[k] for k in "ident_sb row0_sb top_gate top_row".split())
    SLOTS = 4 * P
    ST = SLOTS // P
    HALVES = CAP // P
    UNITS = NB * HALVES // ST
    COLS = NB * HALVES

    def sb(name, shape, dt=F32):
        return ctx.enter_context(nc.sbuf_tensor(name, shape, dt))

    def ps(name, shape):
        return ctx.enter_context(nc.psum_tensor(name, shape, F32))

    def sem(name):
        return ctx.enter_context(nc.semaphore(name))

    row_f = sb("row_f", [BE, CAP])
    rows_all = sb("rows_all", [P, E, NB, HALVES], U32)
    gates_all = sb("gates_all", [P, E, NB, HALVES])
    rows_flat = rows_all[:, :, :, :].rearrange("p e b h -> p (e b h)")
    gates_flat = gates_all[:, :, :, :].rearrange("p e b h -> p (e b h)")
    rows_now = [sb(f"rows_now{i}", [P, ST], U32) for i in range(UNITS)]
    shapes = ([P, DC, F], [P, DC, F], [P, FC, D])
    w_raw = [sb(f"w_raw{i}", s) for i, s in enumerate(shapes)]
    w_hi = [[sb(f"we_hi{k}{i}", s, F32R) for i, s in enumerate(shapes)] for k in range(2)]
    w_lo = [[sb(f"we_lo{k}{i}", s, F32R) for i, s in enumerate(shapes)] for k in range(2)]
    GATE, UP, DOWN = range(3)
    WEIGHTS = len(shapes)
    xs = [sb(f"xs{i}", [P, ST, D]) for i in range(2)]
    x_hi, x_lo = sb("x_hi", [P, DC, SLOTS], F32R), sb("x_lo", [P, DC, SLOTS], F32R)
    silu = [sb(f"silu{i}", [P, SLOTS]) for i in range(2)]
    h = [sb(f"h{i}", [P, SLOTS]) for i in range(2)]
    h_hi, h_lo = sb("h_hi", [P, FC, SLOTS], F32R), sb("h_lo", [P, FC, SLOTS], F32R)
    y = [[sb(f"y{i}{t}", [P, D]) for t in range(ST)] for i in range(2)]

    g_ps = [ps(f"g_ps{i}", [P, SLOTS]) for i in range(2)]
    u_ps = [ps(f"u_ps{i}", [P, SLOTS]) for i in range(2)]
    xt_ps = [ps(f"xt_ps{i}", [P, SLOTS]) for i in range(DC)]
    d_ps = [ps(f"d_ps{i}", [P, SLOTS]) for i in range(2)]

    def rows_ps(t):
        return (d_ps[0], d_ps[1], g_ps[(FC - 1) % 2], u_ps[(FC - 1) % 2])[t][:, 0:D]

    row_cast, row_added, top_turned, top_spread = (
        sem(n) for n in ("row_cast", "row_added", "top_turned", "top_spread"))
    w_in, w_high, w_split = sem("w_in"), sem("w_high"), sem("w_split")
    rows_set = sem("rows_set")
    gathered = [sem(f"gathered{i}") for i in range(2)]
    scattered = [sem(f"scattered{i}") for i in range(UNITS)]
    xt_full, x_high, x_split = sem("xt_full"), sem("x_high"), sem("x_split")
    gate_full, up_full, silu_done, h_done, h_high, h_split = (
        sem(n) for n in ("gate_full", "up_full", "silu_done", "h_done", "h_high", "h_split"))
    down_full, y_scaled = sem("down_full"), sem("y_scaled")
    passed = sem("passed_e")

    def need(eng, s, value):
        if not isinstance(value, int) or value > 0:
            eng.wait_ge(s, value)

    def hold(eng, s, value):
        need(eng, s, value)
        if not isinstance(value, int):
            eng.sem_inc(passed, 1)

    def experts(eng, pair):
        pair(0, False)
        with eng.Fori(1, E // 2 - 1) as p:
            pair(p, False)
        pair(E // 2 - 1, True)

    block = ctx.enter_context(nc.Block())

    @block.sync
    def _(sp):
        def load(e):
            for raw, dram in zip(w_raw, (wg, wu, wd)):
                sp.dma_start(raw[:, :, :], dram[e].rearrange("(c p) n -> p c n", p=P)).then_inc(w_in, DMA)

        def pair(p, last):
            for k in range(2):
                if not (last and k == 1):
                    hold(sp, w_split, WEIGHTS * (2 * p + k + 1))
                    load(2 * p + k + 1)

        load(0)
        experts(sp, pair)

    @block.gpsimd
    def _(pool):
        def gather(e, bp, par):
            unit = UNITS * e + bp
            need(pool, scattered[bp], ST * DMA * e)
            hold(pool, xt_full, DC * (unit - 1))
            pool.tensor_copy(rows_now[bp][:, :], rows_flat[:, bass.ds(e * COLS + bp * ST, ST)]).then_inc(rows_set, 1)
            hold(pool, rows_set, unit + 1)
            for t in range(ST):
                pool.indirect_dma_start(xs[par][:, t, :], None, xn_dram[:, :],
                                        bass.IndirectOffsetOnAxis(ap=rows_now[bp][:, t:t + 1], axis=0))\
                    .then_inc(gathered[par], DMA)

        def scatter(e, bp, par):
            unit = UNITS * e + bp
            for t in range(ST):
                hold(pool, y_scaled, ST * unit + t + 1)
                pool.indirect_dma_start(out[:, :], bass.IndirectOffsetOnAxis(ap=rows_now[bp][:, t:t + 1], axis=0),
                                        y[par][t][:, :], None, compute_op=ALU.add)\
                    .then_inc(scattered[bp], DMA)

        def pair(p, last):
            for k in range(2):
                for bp in range(UNITS):
                    e, n = 2 * p + k, k * UNITS + bp
                    if not (last and n == 2 * UNITS - 1):
                        gather(e + (bp + 1) // UNITS, (bp + 1) % UNITS, (n + 1) % 2)
                    scatter(e, bp, n % 2)

        pool.wait_ge(top_spread, 2 * HALVES)
        gather(0, 0, 0)
        experts(pool, pair)
        for bp in range(UNITS):
            pool.wait_ge(scattered[bp], ST * DMA * E)

    @block.scalar
    def _(act):
        def split_w(e, k, m):
            act.wait_ge(w_in, 3 * DMA * (e + 1))
            act.copy(w_hi[k][m][:, :, :], w_raw[m][:, :, :]).then_inc(w_high, 1)

        def turned(unit):
            for c in range(DC):
                act.wait_ge(xt_full, DC * unit + c + 1)
                act.copy(x_hi[:, c, :], xt_ps[c][:, :]).then_inc(x_high, 1)

        def high(unit, f):
            act.wait_ge(h_done, FC * unit + f + 1)
            act.copy(h_hi[:, f, :], h[f % 2][:, :]).then_inc(h_high, 1)

        def pair(p, last):
            for k in range(2):
                for bp in range(UNITS):
                    unit = UNITS * (2 * p + k) + bp
                    for f in range(FC):
                        act.wait_ge(gate_full, FC * unit + f + 1)
                        act.activation(silu[f % 2][:, :], g_ps[f % 2][:, :], ACT.Silu).then_inc(silu_done, 1)
                        if f > 0:
                            high(unit, f - 1)
                    high(unit, FC - 1)
                    if not (last and k == 1 and bp == UNITS - 1):
                        turned(unit + 1)
                    if bp < WEIGHTS and not (last and k == 1):
                        split_w(2 * p + k + 1, 1 - k, bp)

        turned(0)
        for m in range(WEIGHTS):
            split_w(0, 0, m)
        experts(act, pair)

    @block.tensor
    def _(pe):
        def turn(unit, par):
            pe.wait_ge(gathered[par], ST * DMA * ((unit - par) // 2 + 1) if isinstance(unit, int)
                       else (unit - par) * (ST * DMA // 2) + ST * DMA)
            for c in range(DC):
                need(pe, x_split, DC * unit + c - 1)
                for t in range(ST):
                    last = pe.transpose(xt_ps[c][:, t * P:(t + 1) * P], xs[par][:, t, c * P:(c + 1) * P], ident_sb[:, :])
                last.then_inc(xt_full, 1)

        def gate_up(unit, k):
            pe.wait_ge(x_split, DC * unit + DC)
            for f in range(FC):
                need(pe, h_done, FC * unit + f - 1)
                if f == (FC - 1) % 2:
                    need(pe, y_scaled, ST * unit)
                for w, bank, full in ((GATE, g_ps, gate_full), (UP, u_ps, up_full)):
                    for i, (wt, xt) in enumerate(((w_hi, x_hi), (w_lo, x_hi), (w_hi, x_lo))):
                        for c in range(DC):
                            last = pe.matmul(bank[f % 2][:, :], wt[k][w][:, c, f * P:(f + 1) * P], xt[:, c, :],
                                             start=i == 0 and c == 0, stop=i == 2 and c == DC - 1)
                    last.then_inc(full, 1)

        def down(unit, k):
            def part(t, fs):
                for f in fs:
                    pe.wait_ge(h_split, FC * unit + f + 1)
                    for i, (ht, wt) in enumerate(((h_hi, w_hi), (h_lo, w_hi), (h_hi, w_lo))):
                        last = pe.matmul(rows_ps(t), ht[:, f, t * P:(t + 1) * P], wt[k][DOWN][:, f, :],
                                         start=i == 0 and f == 0, stop=i == 2 and f == FC - 1)
                return last

            for t in range(2):
                need(pe, y_scaled, ST * (unit - 1) + t + 1)
                part(t, range(FC - 1))
            for t in range(2):
                part(t, (FC - 1,)).then_inc(down_full, 1)
            for t in range(2, ST):
                part(t, range(FC)).then_inc(down_full, 1)

        def pair(p, last):
            for k in range(2):
                for bp in range(UNITS):
                    e, n = 2 * p + k, k * UNITS + bp
                    unit = UNITS * e + bp
                    if bp == 0:
                        pe.wait_ge(w_split, WEIGHTS * (e + 1))
                    gate_up(unit, k)
                    if not (last and n == 2 * UNITS - 1):
                        turn(unit + 1, (n + 1) % 2)
                    down(unit, k)

        pe.wait_ge(row_added, 1)
        for i, src in enumerate((row_f, top_gate)):
            for half in range(HALVES):
                last = pe.transpose(d_ps[i][:, half * BE:(half + 1) * BE], src[:, half * P:(half + 1) * P],
                                    ident_sb[0:BE, 0:BE])
        last.then_inc(top_turned, 1)
        turn(0, 0)
        experts(pe, pair)

    @block.vector
    def _(dve):
        def split_w(e, k, m):
            dve.wait_ge(w_high, WEIGHTS * e + m + 1)
            dve.tensor_tensor(w_lo[k][m][:, :, :], w_raw[m][:, :, :], w_hi[k][m][:, :, :], ALU.subtract)\
               .then_inc(w_split, 1)

        def turned(unit):
            for c in range(DC):
                dve.wait_ge(x_high, DC * unit + c + 1)
                dve.tensor_tensor(x_lo[:, c, :], xt_ps[c][:, :], x_hi[:, c, :], ALU.subtract).then_inc(x_split, 1)

        def low(unit, f):
            dve.wait_ge(h_high, FC * unit + f + 1)
            dve.tensor_tensor(h_lo[:, f, :], h[f % 2][:, :], h_hi[:, f, :], ALU.subtract).then_inc(h_split, 1)

        def pair(p, last):
            for k in range(2):
                for bp in range(UNITS):
                    e, n = 2 * p + k, k * UNITS + bp
                    unit = UNITS * e + bp
                    for f in range(FC):
                        dve.wait_ge(silu_done, FC * unit + f + 1)
                        dve.wait_ge(up_full, FC * unit + f + 1)
                        need(dve, h_split, FC * unit + f - 1)
                        dve.tensor_tensor(h[f % 2][:, :], u_ps[f % 2][:, :], silu[f % 2][:, :], ALU.mult)\
                           .then_inc(h_done, 1)
                        if f > 0:
                            low(unit, f - 1)
                    low(unit, FC - 1)
                    if not (last and n == 2 * UNITS - 1):
                        turned(unit + 1)
                    need(dve, scattered[(bp - 2) % UNITS], ST * DMA * (e + (bp >= 2)))
                    for t in range(ST):
                        dve.wait_ge(down_full, ST * unit + t + 1)
                        dve.tensor_scalar(y[n % 2][t][:, :], rows_ps(t),
                                          gates_flat[:, bass.ds(e * COLS + bp * ST + t, 1)], None, ALU.mult)\
                           .then_inc(y_scaled, 1)
                    if bp < WEIGHTS and not (last and k == 1):
                        split_w(e + 1, 1 - k, bp)

        dve.tensor_copy(row_f[:, :], top_row[:, :]).then_inc(row_cast, 1)
        dve.wait_ge(row_cast, 1)
        dve.tensor_scalar(row_f[:, :], row_f[:, :], row0_sb[:, :], None, ALU.add).then_inc(row_added, 1)
        dve.wait_ge(top_turned, 1)
        for i, to in enumerate((rows_all, gates_all)):
            for half in range(HALVES):
                dve.tensor_copy(to[:, :, :, half], d_ps[i][:, half * BE:(half + 1) * BE]
                                .rearrange("p (b e) -> p e b", e=E)).then_inc(top_spread, 1)
        dve.wait_ge(top_spread, 2 * HALVES)
        turned(0)
        for m in range(WEIGHTS):
            split_w(0, 0, m)
        experts(dve, pair)


def kernel(**inputs):
    import numpy as np
    import concourse.bacc as bacc
    from concourse.bass_utils import run_bass_kernel_spmd as run

    x = np.ascontiguousarray(inputs["L0_attn_x"])
    NB, S, D = x.shape
    HD = D // NHEAD
    order = np.arange(D).reshape(NHEAD, HD // 2, 2).transpose(2, 1, 0).reshape(D)
    inv_freq = np.float32(1.0) / np.float32(10000.0) ** (np.arange(0, HD, 2, dtype=np.float32) / np.float32(HD))
    angle = np.outer(np.arange(S, dtype=np.float32), inv_freq).astype(np.float32)

    def columns(v):
        return v.reshape(-1, P).T

    arrays = {
        "x": x.reshape(NB * S, D),
        "ln_w": columns(inputs["L0_attn_ln_w"]), "ln_b": columns(inputs["L0_attn_ln_b"]),
        "wq_t": inputs["L0_attn_Wq"].T[:, order], "wk_t": inputs["L0_attn_Wk"].T[:, order],
        "wv_t": inputs["L0_attn_Wv"].T, "wo_t": inputs["L0_attn_Wo"].T,
        "bq": columns(inputs["L0_attn_bq"][order]), "bk": columns(inputs["L0_attn_bk"][order]),
        "bv": inputs["L0_attn_bv"], "bo": inputs["L0_attn_bo"],
        "gate_w": inputs["L0_ffn_gate_w"],
        "wg": inputs["L0_ffn_Wg"], "wu": inputs["L0_ffn_Wu"], "wd": inputs["L0_ffn_Wd"],
        "cos": np.repeat(np.cos(angle).T, NHEAD, axis=0), "sin": np.repeat(np.sin(angle).T, NHEAD, axis=0),
        "ident": np.eye(P, dtype=np.float32),
        "heads": (np.arange(P)[:, None] % NHEAD == np.arange(KEYS_W)[None, :]).astype(np.float32),
        "row0": np.repeat(np.arange(NB, dtype=np.float32) * S, NEXPERT)[:, None],
    }
    arrays = {k: np.ascontiguousarray(v) for k, v in arrays.items()}
    nc = bacc.Bacc("TRN2", target_bir_lowering=False, num_devices=1)
    args = {k: nc.dram_tensor(f"in_{k}", v.shape, mybir.dt.from_np(v.dtype), kind="ExternalInput").ap()
            for k, v in arrays.items()}
    out = nc.dram_tensor("out_0", (NB * S, D), F32, kind="ExternalOutput").ap()
    build(nc, **args, out=out)
    r = run(nc, [{f"in_{k}": v for k, v in arrays.items()}], core_ids=[0])
    return r.results[0]["out_0"].reshape(NB, S, D)
```
